# Optimizing a Trainium2 kernel written in Bass

```python
import numpy as np
import jax
import jax.numpy as jnp

def _softmax(x, axis=-1):
    return jax.nn.softmax(x, axis=axis)

def _gelu(x):
    return jax.nn.gelu(x, approximate=True)

def _silu(x):
    return jax.nn.silu(x)

def _sigmoid(x):
    return jax.nn.sigmoid(x)

def _layernorm(x, axis=-1, eps=1e-05):
    m = jnp.mean(x, axis=axis, keepdims=True)
    v = jnp.var(x, axis=axis, keepdims=True)
    return (x - m) / jnp.sqrt(v + eps)

def _scatter_add(tgt, idx, src, axis=0):
    return tgt.at[idx].add(src)

def _segment_sum(src, seg, n):
    return jax.ops.segment_sum(src, seg, n)
kernel_name = 'mk_seq_postln_d1_jaxref_r4_309a5f'

def setup_inputs(seed: int=0):
    np.random.seed(seed)
    _w = jnp.asarray

    def _L0_attn_setup():
        import jax, jax.numpy as jnp
        import numpy as np
        D_MODEL, D_STATE, D_CONV = (256, 16, 4)
        B_, L_ = (4, 512)
        LN_EPS = 1e-05

        def _silu(v):
            return v * jax.nn.sigmoid(v)

        def _mamba_fwd(x, in_proj_w, in_proj_b, conv_w, conv_b, bc_w, bc_b, dt_w, dt_b, A_log, D, out_w, out_b, ln_g, ln_b):
            b, l, d = x.shape
            x_proj = x @ in_proj_w.T + in_proj_b
            x_ssm, x_gate = jnp.split(x_proj, 2, axis=-1)
            xc = lax.conv_general_dilated(x_ssm.transpose(0, 2, 1), conv_w, window_strides=(1,), padding=[(D_CONV - 1, 0)], feature_group_count=d, dimension_numbers=('NCH', 'OIH', 'NCH'))
            x_conv = _silu((xc + conv_b[None, :, None]).transpose(0, 2, 1))
            BC = x_conv @ bc_w.T + bc_b
            Bm, Cm = jnp.split(BC, 2, axis=-1)
            dt = jax.nn.softplus(x_conv @ dt_w.T + dt_b)
            A = -jnp.exp(A_log)

            def step(h, inp):
                xt, dtt, Bt, Ct = inp
                dA = jnp.exp(dtt[:, :, None] * A)
                dB = dtt[:, :, None] * Bt[:, None, :]
                h = h * dA + dB * xt[:, :, None]
                y = jnp.einsum('bdn,bn->bd', h, Ct) + xt * D
                return (h, y)
            h0 = jnp.zeros((b, d, D_STATE), x.dtype)
            xs = (x_conv.transpose(1, 0, 2), dt.transpose(1, 0, 2), Bm.transpose(1, 0, 2), Cm.transpose(1, 0, 2))
            _, ys = lax.scan(step, h0, xs)
            y = ys.transpose(1, 0, 2)
            y = y * _silu(x_gate)
            out = y @ out_w.T + out_b
            z = out + x
            mu = jnp.mean(z, axis=-1, keepdims=True)
            var = jnp.var(z, axis=-1, keepdims=True)
            return (z - mu) * jax.lax.rsqrt(var + LN_EPS) * ln_g + ln_b
        from jax import lax
        key = jax.random.key(seed)
        ks = jax.random.split(key, 16)
        s = 0.02
        return {'x': jax.random.normal(ks[0], (B_, L_, D_MODEL), jnp.float32), 'in_proj_w': jax.random.normal(ks[1], (2 * D_MODEL, D_MODEL), jnp.float32) * s, 'in_proj_b': jnp.zeros((2 * D_MODEL,), jnp.float32), 'conv_w': jax.random.normal(ks[2], (D_MODEL, 1, D_CONV), jnp.float32) * s, 'conv_b': jnp.zeros((D_MODEL,), jnp.float32), 'bc_w': jax.random.normal(ks[3], (2 * D_STATE, D_MODEL), jnp.float32) * s, 'bc_b': jnp.zeros((2 * D_STATE,), jnp.float32), 'dt_w': jax.random.normal(ks[4], (D_MODEL, D_MODEL), jnp.float32) * s, 'dt_b': jnp.zeros((D_MODEL,), jnp.float32), 'A_log': jax.random.normal(ks[5], (D_MODEL, D_STATE), jnp.float32), 'D': jnp.ones((D_MODEL,), jnp.float32), 'out_w': jax.random.normal(ks[6], (D_MODEL, D_MODEL), jnp.float32) * s, 'out_b': jnp.zeros((D_MODEL,), jnp.float32), 'ln_g': jnp.ones((D_MODEL,), jnp.float32), 'ln_b': jnp.zeros((D_MODEL,), jnp.float32)}
    _L0_attn_in = _L0_attn_setup()

    def _L0_ffn_setup():
        import jax, jax.numpy as jnp
        import numpy as np
        SWIGLU_ALPHA = 1.702
        SWIGLU_LIMIT = 7.0
        TOP_K = 4
        key = jax.random.key(seed)
        k = jax.random.split(key, 5)
        B, S, D, E, I = (2, 256, 256, 8, 512)
        return {'hidden_states': jax.random.normal(k[0], (B, S, D), dtype=jnp.float32), 'router_weight': jax.random.normal(k[1], (E, D), dtype=jnp.float32) * 0.02, 'router_bias': jnp.zeros((E,), dtype=jnp.float32), 'gate_up_proj': jax.random.normal(k[2], (E, 2 * I, D), dtype=jnp.float32) * 0.02, 'gate_up_proj_bias': jnp.zeros((E, 2 * I), dtype=jnp.float32), 'down_proj': jax.random.normal(k[3], (E, D, I), dtype=jnp.float32) * 0.02, 'down_proj_bias': jnp.zeros((E, D), dtype=jnp.float32)}
    _L0_ffn_in = _L0_ffn_setup()
    _d = {'L0_attn_x': _L0_attn_in['x'], 'L0_attn_in_proj_w': _L0_attn_in['in_proj_w'], 'L0_attn_in_proj_b': _L0_attn_in['in_proj_b'], 'L0_attn_conv_w': _L0_attn_in['conv_w'], 'L0_attn_conv_b': _L0_attn_in['conv_b'], 'L0_attn_bc_w': _L0_attn_in['bc_w'], 'L0_attn_bc_b': _L0_attn_in['bc_b'], 'L0_attn_dt_w': _L0_attn_in['dt_w'], 'L0_attn_dt_b': _L0_attn_in['dt_b'], 'L0_attn_A_log': _L0_attn_in['A_log'], 'L0_attn_D': _L0_attn_in['D'], 'L0_attn_out_w': _L0_attn_in['out_w'], 'L0_attn_out_b': _L0_attn_in['out_b'], 'L0_attn_ln_g': _L0_attn_in['ln_g'], 'L0_attn_ln_b': _L0_attn_in['ln_b'], 'L0_ffn_router_weight': _L0_ffn_in['router_weight'], 'L0_ffn_router_bias': _L0_ffn_in['router_bias'], 'L0_ffn_gate_up_proj': _L0_ffn_in['gate_up_proj'], 'L0_ffn_gate_up_proj_bias': _L0_ffn_in['gate_up_proj_bias'], 'L0_ffn_down_proj': _L0_ffn_in['down_proj'], 'L0_ffn_down_proj_bias': _L0_ffn_in['down_proj_bias']}
    _x0 = _d['L0_attn_x']
    _d['L0_attn_x'] = jax.random.normal(jax.random.fold_in(jax.random.key(seed), 1), (8, 512, 256), dtype=_x0.dtype)
    del _x0
    return _d

def reference(L0_attn_x, L0_attn_in_proj_w, L0_attn_in_proj_b, L0_attn_conv_w, L0_attn_conv_b, L0_attn_bc_w, L0_attn_bc_b, L0_attn_dt_w, L0_attn_dt_b, L0_attn_A_log, L0_attn_D, L0_attn_out_w, L0_attn_out_b, L0_attn_ln_g, L0_attn_ln_b, L0_ffn_router_weight, L0_ffn_router_bias, L0_ffn_gate_up_proj, L0_ffn_gate_up_proj_bias, L0_ffn_down_proj, L0_ffn_down_proj_bias):

    def _L0_attn_ref(x, in_proj_w, in_proj_b, conv_w, conv_b, bc_w, bc_b, dt_w, dt_b, A_log, D, out_w, out_b, ln_g, ln_b):
        import jax, jax.numpy as jnp
        import numpy as np
        D_MODEL, D_STATE, D_CONV = (256, 16, 4)
        B_, L_ = (4, 512)
        LN_EPS = 1e-05

        def _silu(v):
            return v * jax.nn.sigmoid(v)

        def _mamba_fwd(x, in_proj_w, in_proj_b, conv_w, conv_b, bc_w, bc_b, dt_w, dt_b, A_log, D, out_w, out_b, ln_g, ln_b):
            b, l, d = x.shape
            x_proj = x @ in_proj_w.T + in_proj_b
            x_ssm, x_gate = jnp.split(x_proj, 2, axis=-1)
            xc = lax.conv_general_dilated(x_ssm.transpose(0, 2, 1), conv_w, window_strides=(1,), padding=[(D_CONV - 1, 0)], feature_group_count=d, dimension_numbers=('NCH', 'OIH', 'NCH'))
            x_conv = _silu((xc + conv_b[None, :, None]).transpose(0, 2, 1))
            BC = x_conv @ bc_w.T + bc_b
            Bm, Cm = jnp.split(BC, 2, axis=-1)
            dt = jax.nn.softplus(x_conv @ dt_w.T + dt_b)
            A = -jnp.exp(A_log)

            def step(h, inp):
                xt, dtt, Bt, Ct = inp
                dA = jnp.exp(dtt[:, :, None] * A)
                dB = dtt[:, :, None] * Bt[:, None, :]
                h = h * dA + dB * xt[:, :, None]
                y = jnp.einsum('bdn,bn->bd', h, Ct) + xt * D
                return (h, y)
            h0 = jnp.zeros((b, d, D_STATE), x.dtype)
            xs = (x_conv.transpose(1, 0, 2), dt.transpose(1, 0, 2), Bm.transpose(1, 0, 2), Cm.transpose(1, 0, 2))
            _, ys = lax.scan(step, h0, xs)
            y = ys.transpose(1, 0, 2)
            y = y * _silu(x_gate)
            out = y @ out_w.T + out_b
            z = out + x
            mu = jnp.mean(z, axis=-1, keepdims=True)
            var = jnp.var(z, axis=-1, keepdims=True)
            return (z - mu) * jax.lax.rsqrt(var + LN_EPS) * ln_g + ln_b
        from jax import lax
        return _mamba_fwd(x, in_proj_w, in_proj_b, conv_w, conv_b, bc_w, bc_b, dt_w, dt_b, A_log, D, out_w, out_b, ln_g, ln_b)

    def _L0_ffn_ref(hidden_states, router_weight, router_bias, gate_up_proj, gate_up_proj_bias, down_proj, down_proj_bias):
        import jax, jax.numpy as jnp
        import numpy as np
        SWIGLU_ALPHA = 1.702
        SWIGLU_LIMIT = 7.0
        TOP_K = 4
        B, S, D = hidden_states.shape
        E = router_weight.shape[0]
        x = hidden_states.reshape(-1, D)
        N = x.shape[0]
        logits = x @ router_weight.T + router_bias
        topk_logits, topk_idx = jax.lax.top_k(logits, TOP_K)
        topk_w = jax.nn.softmax(topk_logits.astype(jnp.float32), axis=-1)
        combine = jnp.zeros((N, E), dtype=jnp.float32)
        combine = combine.at[jnp.arange(N)[:, None], topk_idx].set(topk_w)
        gate_up = jnp.einsum('nd,ejd->nej', x, gate_up_proj) + gate_up_proj_bias
        gate, up = jnp.split(gate_up, 2, axis=-1)
        gate = jnp.minimum(gate, SWIGLU_LIMIT)
        up = jnp.clip(up, -SWIGLU_LIMIT, SWIGLU_LIMIT)
        act = (up + 1.0) * gate * jax.nn.sigmoid(SWIGLU_ALPHA * gate)
        out = jnp.einsum('nei,edi->ned', act, down_proj) + down_proj_bias
        y = jnp.einsum('ned,ne->nd', out, combine.astype(out.dtype))
        return y.reshape(B, S, D)
    x = L0_attn_x
    x = _layernorm(x + _L0_attn_ref(x, L0_attn_in_proj_w, L0_attn_in_proj_b, L0_attn_conv_w, L0_attn_conv_b, L0_attn_bc_w, L0_attn_bc_b, L0_attn_dt_w, L0_attn_dt_b, L0_attn_A_log, L0_attn_D, L0_attn_out_w, L0_attn_out_b, L0_attn_ln_g, L0_attn_ln_b), axis=-1)
    x = _layernorm(x + _L0_ffn_ref(x, L0_ffn_router_weight, L0_ffn_router_bias, L0_ffn_gate_up_proj, L0_ffn_gate_up_proj_bias, L0_ffn_down_proj, L0_ffn_down_proj_bias), axis=-1)
    return x

_drawn_inputs = setup_inputs


def setup_inputs(seed=0):
    import zlib

    import numpy as np

    out = dict(_drawn_inputs(seed))
    spreads = {'L0_attn_in_proj_b': (0.0, 0.8),
     'L0_attn_conv_b': (0.0, 0.8),
     'L0_attn_bc_b': (0.0, 0.8),
     'L0_attn_dt_b': (0.0, 0.8),
     'L0_attn_D': (1.0, 0.6),
     'L0_attn_out_b': (0.0, 0.1),
     'L0_attn_ln_g': (1.0, 0.2),
     'L0_attn_ln_b': (0.0, 0.1),
     'L0_ffn_router_bias': (0.0, 0.323),
     'L0_ffn_gate_up_proj_bias': (0.0, 0.574),
     'L0_ffn_down_proj_bias': (0.0, 0.1)}
    factors = {'L0_attn_in_proj_w': 8.0,
     'L0_attn_conv_w': 8.0,
     'L0_attn_bc_w': 8.0,
     'L0_attn_dt_w': 8.0,
     'L0_attn_A_log': 8.0,
     'L0_attn_out_w': 8.0}
    for name, (base, spread) in spreads.items():
        noise = np.random.default_rng([zlib.crc32(name.encode()), seed]).standard_normal(out[name].shape)
        drawn = base * np.exp(spread * noise) if base else spread * noise
        out[name] = jnp.asarray(drawn.astype(out[name].dtype))
    for name, factor in factors.items():
        out[name] = (out[name] * factor).astype(out[name].dtype)
    return out
```

```python
from contextlib import ExitStack

import numpy as np

import concourse.bass as bass
from concourse import mybir

F32 = mybir.dt.float32
F32R = mybir.dt.float32r
BF16 = mybir.dt.bfloat16
U32 = mybir.dt.uint32
I32 = mybir.dt.int32
ALU = mybir.AluOpType
ACT = mybir.ActivationFunctionType
AX = mybir.AxisListType

P = 128
SEQS, LEN, D = 8, 512, 256
TOKENS = SEQS * LEN
STATE, TAPS = 16, 4
HALVES = D // P
CHPG = P // STATE
GROUPS = D // CHPG
QUADS = GROUPS // 4
SLOTS = GROUPS // 2
TT = LEN // P
EPS = 1e-5
E, TOPK, INNER = 8, 4, 512
ALPHA, LIMIT = 1.702, 7.0
TILE = 512
SUBS = TILE // P
ROW = 272
COL_TOKEN, COL_WEIGHT = D, D + 1
QUEUE = TOKENS + TILE
CH = INNER // P
KD = D // P
W_GU, W_D, W_B = KD * 2 * INNER, CH * D, 2 * CH + D
W_ALL = W_GU + W_D + W_B


class Seq:

    def __init__(self, half, off):
        self.off, self.half = off, half
        self.n = 2 * half + off
        self.p = off % 2
        self.use = half + off // 2

    def at(self, d):
        return Seq(self.half, self.off + d)


class Round:
    FIRST, LAST = -1, SEQS + 1
    LOOP = range(3, SEQS - 1)

    def __init__(self, seq, like):
        self.s, self.like = seq, like
        self.a = like + 1 < SEQS
        self.b = 0 <= like < SEQS
        self.c = 0 <= like - 1 < SEQS
        self.d = 0 <= like - 2 < SEQS

    def blocks(self):
        d, a, c = self.d, self.a, self.c
        return (["tr0", "tr1", "rt"] * d + ["in0", "in1", "cv0", "cv1", "in2", "in3"] * a + ["cnt"] * d
                + ["o0", "o1"] * c + ["dt0", "dt1", "bb", "cc"] * a)

    def block(self, name):
        before = sum(len(Round(Seq(0, i), i).blocks()) for i in range(Round.FIRST, self.like))
        k = before + self.blocks().index(name)
        per = len(self.blocks()) // 2
        return k % 2, k // 2 + 1 + (0 if isinstance(self.s.half, int) else per * (self.s.n - self.like))


def rounds(eng):
    lo, hi = Round.LOOP.start, Round.LOOP.stop
    for i in range(Round.FIRST, lo):
        yield Round(Seq(0, i), i)
    with eng.Fori(lo // 2, hi // 2) as half:
        for off in range(2):
            yield Round(Seq(half, lo % 2 + off), lo + off)
    for i in range(hi, Round.LAST + 1):
        yield Round(Seq(0, i), i)


def constants():
    p = np.arange(P)
    col = np.arange(P)
    c = {}
    c["pick"] = (p[:, None, None] % 64 == CHPG * np.arange(8)[None, :, None] + col[None, None, :] // STATE)
    c["gather"] = np.arange(32)[None, None, :] == CHPG * np.arange(4)[None, :, None] + p[:, None, None] // STATE
    c["ident"] = p[:, None] == col[None, :]
    c["before"] = p[:, None] < col[None, :]
    c["ones"] = np.ones((P, P))
    e = np.arange(E)
    c["lower"] = np.broadcast_to(e[None, :] < e[:, None], (P, E, E))
    c["upper"] = np.broadcast_to(e[None, :] > e[:, None], (P, E, E))
    c["slot"] = np.broadcast_to(np.arange(TOPK)[:, None], (P, TOPK, E))
    c["queue"] = np.broadcast_to(e * QUEUE, (P, E))
    c["token"] = p[:, None] + P * np.arange(TT)[None, :]
    c["spill"] = TOKENS + SUBS * p[:, None] + np.arange(SUBS)[None, :]
    c["tile"] = np.broadcast_to(np.arange(PLANNED)[:, None], (P, PLANNED, E))
    return {k: np.ascontiguousarray(np.broadcast_to(v, v.shape), dtype=np.float32).reshape(P, -1) for k, v in c.items()}


TILES = TOKENS * TOPK // TILE + E
PLANNED = TILES + 2
CONSTANTS = constants()


class Steps:

    def __init__(self, eng, sem, use, per):
        self.eng, self.sem, self.base, self.per, self.k = eng, sem, use * per, per, 0

    def then(self, ins):
        self.k += 1
        ins.then_inc(self.sem, 1)
        self.eng.wait_ge(self.sem, self.base + self.k)

    def last(self, ins):
        self.k += 1
        ins.then_inc(self.sem, 1)
        assert self.k == self.per, self.k


def program(nc, ins, out):
    with ExitStack() as ctx:
        build(nc, ctx, ins, out)


def build(nc, ctx, ins, out):
    def sem(name):
        return ctx.enter_context(nc.semaphore(name))

    def sb(name, *shape, dt=F32, at=ctx):
        return at.enter_context(nc.sbuf_tensor(name, [P, *shape], dt))

    def ps(name, cols, at=ctx):
        return at.enter_context(nc.psum_tensor(name, [P, cols], F32))

    queues = nc.dram_tensor("queues", [E * QUEUE + TILE, ROW], F32).ap()
    total = nc.dram_tensor("total", [TOKENS + TILE, D], F32).ap()
    total_rows = total[0:TOKENS, :].rearrange("(s t p) d -> s p t d", t=TT, p=P)
    out_rows = out.rearrange("s (t p) d -> s p t d", p=P)

    ident = sb("ident", P)
    base = sb("base", E)
    c_queue = sb("c_queue", E)
    c_spill = sb("c_spill", SUBS)
    scrap = sb("scrap", 2)
    neg_half = sb("neg_half", TT)


    one = ctx.enter_context(ExitStack())
    NW = 2 * D + D + D + 2 * STATE
    IN, DT_, OUT, BC = 0, 2 * D, 3 * D, 4 * D
    w_hi = sb("w_hi", KD, NW, dt=F32R, at=one)
    w_lo = sb("w_lo", KD, NW, dt=F32R, at=one)
    bc_hi = sb("bc_hi", KD, 2, P, dt=F32R, at=one)
    bc_lo = sb("bc_lo", KD, 2, P, dt=F32R, at=one)
    pick = sb("pick", 8, P, dt=F32R, at=one)
    gather = sb("gather", 4, 32, at=one)
    taps = sb("taps", HALVES * TAPS, P, at=one)
    tap = sb("tap", HALVES * TAPS, at=one)
    wr = sb("wr", KD, E, at=one)
    rate = sb("rate", GROUPS, at=one)
    b_in = sb("b_in", 4, at=one)
    b_conv = sb("b_conv", HALVES, at=one)
    b_dt = sb("b_dt", HALVES, at=one)
    skip = sb("skip", HALVES, at=one)
    b_bc = sb("b_bc", 2, at=one)
    bo_hi = sb("bo_hi", D, dt=F32R, at=one)
    bo_lo = sb("bo_lo", D, dt=F32R, at=one)
    ones_r = sb("ones_r", P, dt=F32R, at=one)
    ln_g = sb("ln_g", D, at=one)
    ln_b = sb("ln_b", D, at=one)
    b_router = sb("b_router", E, at=one)
    before = sb("before", P, dt=BF16, at=one)
    ones = sb("ones", P, dt=BF16, at=one)
    lower = sb("lower", E, E, at=one)
    upper = sb("upper", E, E, at=one)
    slot = sb("slot", TOPK, E, at=one)
    token = sb("token", TT, at=one)

    xt = sb("xt", KD, LEN, at=one)
    xt_hi = sb("xt_hi", KD, LEN, dt=F32R, at=one)
    xt_lo = sb("xt_lo", KD, LEN, dt=F32R, at=one)
    x = sb("x", TT, D, at=one)
    xpad = sb("xpad", HALVES, TAPS - 1 + LEN, at=one)
    xc = [sb(f"xc{i}", HALVES, LEN, at=one) for i in range(2)]
    sg = [sb(f"sg{i}", HALVES, LEN, at=one) for i in range(2)]
    xc_hi = sb("xc_hi", KD, LEN, dt=F32R, at=one)
    xc_lo = sb("xc_lo", KD, LEN, dt=F32R, at=one)
    relu = sb("relu", HALVES, LEN, at=one)
    expo = sb("expo", HALVES, LEN, at=one)
    rest = sb("rest", HALVES, LEN, at=one)
    dt_st = [sb(f"dt_st{i}", 2 * HALVES, LEN, dt=F32R, at=one) for i in range(2)]
    u_st = [sb(f"u_st{i}", 2 * HALVES, LEN, dt=F32R, at=one) for i in range(2)]
    b_rep = [sb(f"b_rep{i}", LEN, at=one) for i in range(2)]
    c_rep = [sb(f"c_rep{i}", LEN, at=one) for i in range(2)]
    decay = [sb(f"decay{i}", 4, LEN, at=one) for i in range(2)]
    state = [sb(f"state{i}", 2, LEN, at=one) for i in range(2)]
    read = [sb(f"read{i}", 4, LEN, at=one) for i in range(2)]
    y = sb("y", HALVES, LEN, at=one)
    y_hi = sb("y_hi", HALVES, LEN, dt=F32R, at=one)
    y_lo = sb("y_lo", HALVES, LEN, dt=F32R, at=one)
    z = sb("z", TT, D, at=one)
    stats = sb("stats", 2, TT, 6, at=one)
    mv = sb("mv", 2, TT, 2, at=one)
    rstd = sb("rstd", 2, TT, at=one)
    rows = [sb(f"rows{i}", TT, ROW, at=one) for i in range(2)]
    x1t = sb("x1t", KD, LEN, at=one)
    logp = x1t
    lg = sb("lg", TT, E, at=one)
    cmp = sb("cmp", 2, TT, E, E, at=one)
    rank = sb("rank", TT, E, at=one)
    chosen = sb("chosen", TT + 1, E, dt=BF16, at=one)
    top = sb("top", TT, at=one)
    ex = sb("ex", TT, E, at=one)
    den = sb("den", 2, TT, at=one)
    place = sb("place", TT, E, at=one)
    spot = sb("spot", TT, TOPK, E, at=one)
    spot_sum = sb("spot_sum", TT, TOPK, at=one)
    index = [sb(f"index{i}", TT * TOPK, dt=U32, at=one) for i in range(2)]

    pone = ctx.enter_context(ExitStack())
    p_bank = [ps(f"p_bank{i}", 512, at=pone) for i in range(2)]
    p_dt = ps("p_dt", 512, at=pone)
    p_u = [ps(f"p_u{i}", 1024, at=pone) for i in range(2)]
    p_y = ps("p_y", 512, at=pone)

    s_const, s_raw = sem("s_const"), sem("s_raw")
    s_set_dve, s_set_act, s_set_pool = sem("s_set_dve"), sem("s_set_act"), sem("s_set_pool")
    s_xt, s_x = sem("s_xt"), sem("s_x")
    bank_full = [sem(f"bank_full{i}") for i in range(2)]
    bank_read = [sem(f"bank_read{i}") for i in range(2)]
    s_xt_hi, s_xt_lo, s_silu, s_xc_hi, s_xc_lo = (sem(n) for n in ("s_xt_hi", "s_xt_lo", "s_silu", "s_xc_hi", "s_xc_lo"))
    s_exp, s_log, s_rest0, s_rest, s_sum, s_dt, s_u = (sem(n) for n in ("s_exp", "s_log", "s_rest0", "s_rest", "s_sum", "s_dt", "s_u"))
    s_hi, s_lo = sem("s_hi"), sem("s_lo")
    s_pdt, s_pu, s_decay, s_bu, s_state, s_read, s_quad = (sem(n) for n in ("s_pdt", "s_pu", "s_decay", "s_bu", "s_state", "s_read", "s_quad"))
    s_skip, s_y, s_y_hi, s_y_lo = (sem(n) for n in ("s_skip", "s_y", "s_y_hi", "s_y_lo"))
    s_norm, s_rstd, s_xb, s_scaled, s_x1 = (sem(n) for n in ("s_norm", "s_rstd", "s_xb", "s_scaled", "s_x1"))
    s_route, s_rexp, s_chosen, s_index = (sem(n) for n in ("s_route", "s_rexp", "s_chosen", "s_index"))
    s_scrap = sem("s_scrap")
    s_scat = [sem(f"s_scat{i}") for i in range(2)]
    s_total = [sem(f"s_total{i}") for i in range(2)]
    NORM_STEPS, ROUTE_STEPS = 8, 13

    raw = read[0][:, :, :].rearrange("p a b -> p (a b)")
    raw_w0, raw_w1 = raw[:, 0:NW], read[1][:, :, :].rearrange("p a b -> p (a b)")[:, 0:NW]
    raw_pick = decay[0][:, 0:2, :].rearrange("p a b -> p (a b)")

    c_before, c_ones, b_out = state[0][:, 0, 0:P], state[0][:, 0, P:2 * P], state[0][0:1, 0, 2 * P:2 * P + D]

    loads = []
    def load(to, src):
        loads.append((to, src))
    for k, to in enumerate((raw_w0, raw_w1)):
        for name, at, n in (("w_in_t", IN, 2 * D), ("w_dt_t", DT_, D), ("w_out_t", OUT, D), ("w_bc_t", BC, 2 * STATE)):
            load(to[:, at:at + n], ins[name][k * P:(k + 1) * P, :])
        load(wr[:, k, :], ins["w_router_t"][k * P:(k + 1) * P, :])
    load(raw_pick, ins["pick"])
    load(gather[:, :, :].rearrange("p a b -> p (a b)"), ins["gather"])
    load(ident[:, :], ins["ident"])
    load(c_before, ins["before"])
    load(c_ones, ins["ones"])
    load(lower[:, :, :].rearrange("p a b -> p (a b)"), ins["lower"])
    load(upper[:, :, :].rearrange("p a b -> p (a b)"), ins["upper"])
    load(slot[:, :, :].rearrange("p a b -> p (a b)"), ins["slot"])
    load(base[:, :], ins["queue"])
    load(c_queue[:, :], ins["queue"])
    load(c_spill[:, :], ins["spill"])
    load(token[:, :], ins["token"])
    load(rate[:, :], ins["a_log_rows"])
    load(b_in[:, :], ins["b_in"])
    load(b_conv[:, :], ins["b_conv"])
    load(b_dt[:, :], ins["b_dt"])
    load(skip[:, :], ins["skip"])
    load(b_bc[:, :], ins["b_bc_rows"])
    load(tap[:, :], ins["taps"])
    load(b_out, ins["b_out"])
    load(ln_g[:, :], ins["ln_g"].partition_broadcast(P))
    load(ln_b[:, :], ins["ln_b"].partition_broadcast(P))
    load(b_router[:, :], ins["b_router"].partition_broadcast(P))
    SETUP = 16 * len(loads)

    def after(eng, s, n):
        if not isinstance(n, int) or n > 0:
            eng.wait_ge(s, n)

    def pair_of(t):
        quad = t // 2
        return quad, quad // 4, quad % 4, (2 * (t % 2), 2 * (t % 2) + 1)

    def flat(ap):
        return ap.rearrange("p a b -> p (a b)")

    def full(eng, r, name):
        bank, n = r.block(name)
        eng.wait_ge(bank_full[bank], n)
        return p_bank[bank], bank_read[bank]

    def pe_stage1(pe):
        pe.wait_ge(s_const, SETUP)
        pe.wait_ge(s_set_dve, SET_DVE)

        def block(r, name):
            bank, n = r.block(name)
            after(pe, bank_read[bank], n - 1)
            return p_bank[bank], bank_full[bank]

        def product(out, hi, lo, rhs_hi, rhs_lo, stop=True):
            for k in range(KD):
                for n, (a, b) in enumerate(((hi, rhs_hi), (hi, rhs_lo), (lo, rhs_hi))):
                    mm = pe.matmul(out, a(k), b(k), start=(k == 0 and n == 0),
                                   stop=(k == KD - 1 and n == 2 and stop))
            return mm

        def weight(at, n, part):
            return lambda k: part[:, k, at:at + n]

        def project(r, m):
            bank, done = block(r, f"in{m}")
            if m == 0:
                pe.wait_ge(s_xt_hi, r.s.at(1).n + 1)
                pe.wait_ge(s_xt_lo, r.s.at(1).n + 1)
            at = IN + m * P
            product(bank[:, :], weight(at, P, w_hi), weight(at, P, w_lo),
                    lambda k: xt_hi[:, k, :], lambda k: xt_lo[:, k, :]).then_inc(done, 1)

        def convolve(r, h):
            bank, done = block(r, f"cv{h}")
            src, n = r.block(f"in{h}")
            pe.wait_ge(bank_read[src], n)
            for j in range(TAPS):
                mm = pe.matmul(bank[:, :], taps[:, TAPS * h + j, :], xpad[:, h, j:j + LEN],
                               start=(j == 0), stop=(j == TAPS - 1))
            mm.then_inc(done, 1)

        def from_xc(r, name, hi, lo):
            bank, done = block(r, name)
            if name == "dt0":
                pe.wait_ge(s_xc_hi, r.s.at(1).n + 1)
                pe.wait_ge(s_xc_lo, r.s.at(1).n + 1)
            product(bank[:, :], hi, lo, lambda k: xc_hi[:, k, :], lambda k: xc_lo[:, k, :]).then_inc(done, 1)

        def replicate(r, t):
            s = r.s
            quad, half, j, tiles = pair_of(t)
            if t == 0:
                pe.wait_ge(s_hi, s.n + 1)
                pe.wait_ge(s_lo, s.n + 1)
            q = 2 * half + t % 2
            for i, c in enumerate(tiles):
                which = j + 4 * (c % 2)
                after(pe, s_decay, GROUPS * s.n + 2 * t + i)
                pe.matmul(p_dt[:, :], pick[:, which, :], dt_st[s.p][:, q, :], start=True, stop=True).then_inc(s_pdt, 1)
                if i == 0:
                    after(pe, s_state, SLOTS * s.n + t - 1)
                mm = pe.matmul(p_u[t % 2][:, i * LEN:(i + 1) * LEN], pick[:, which, :], u_st[s.p][:, q, :],
                               start=True, stop=True)
            mm.then_inc(s_pu, 1)

        def sum_states(s, quad):
            half, j = quad // 4, quad % 4
            pe.wait_ge(s_read, SLOTS * s.n + 2 * quad + 2)
            if j == 0:
                after(pe, s_skip, 2 * s.n + half)
            for c in range(4):
                mm = pe.matmul(p_y[32 * c:32 * c + 32, :], gather[:, j, :], read[quad % 2][:, c, :],
                               start=(j == 0), stop=(j == 3))
            mm.then_inc(s_quad, 1)

        def project_out(r, b):
            bank, done = block(r, f"o{b}")
            s = r.s.at(-1)
            if b == 0:
                pe.wait_ge(s_y_hi, s.n + 1)
                pe.wait_ge(s_y_lo, s.n + 1)
            for i in range(2):
                to = bank[:, i * D:(i + 1) * D]
                at = (2 * b + i) * P
                product(to, lambda k: y_hi[:, k, at:at + P], lambda k: y_lo[:, k, at:at + P],
                        lambda k: w_hi[:, k, OUT:OUT + D], lambda k: w_lo[:, k, OUT:OUT + D], stop=False)
                pe.matmul(to, ones_r[0:1, :], bo_hi[0:1, :], start=False, stop=False)
                mm = pe.matmul(to, ones_r[0:1, :], bo_lo[0:1, :], start=False, stop=True)
            mm.then_inc(done, 1)

        def transpose_rows(r, k):
            bank, done = block(r, f"tr{k}")
            s = r.s.at(-2)
            pe.wait_ge(s_x1, s.n + 1)
            for t in range(TT):
                mm = pe.transpose(bank[:, t * P:(t + 1) * P], rows[s.p][:, t, k * P:(k + 1) * P], ident[:, :])
            mm.then_inc(done, 1)

        def route(r):
            bank, done = block(r, "rt")
            for k in range(KD):
                src, n = r.block(f"tr{k}")
                pe.wait_ge(bank_read[src], n)
            for t in range(TT):
                for k in range(KD):
                    mm = pe.matmul(bank[:, t * E:(t + 1) * E], x1t[:, k, t * P:(t + 1) * P], wr[:, k, :],
                                   start=(k == 0), stop=(k == KD - 1))
            mm.then_inc(done, 1)

        def count(r):
            bank, done = block(r, "cnt")
            pe.wait_ge(s_chosen, r.s.at(-2).n + 1)
            pe.matmul(bank[:, 0:(TT + 1) * E], before[:, :], flat(chosen[:, :, :]), start=True, stop=False,
                      skip_group_check=True)
            for t in range(TT):
                n = TT - t
                mm = pe.matmul(bank[:, (t + 1) * E:(TT + 1) * E], ones[:, :],
                               chosen[:, t:t + 1, :].broadcast_to([P, n, E]), start=False, stop=(t == TT - 1),
                               skip_group_check=True)
            mm.then_inc(done, 1)

        for r in rounds(pe):
            for t in range(SLOTS):
                if r.b:
                    replicate(r, t)
                if t in (0, 2) and r.c:
                    sum_states(r.s.at(-1), QUADS - 2 + t // 2)
                if t >= 4 and t % 2 == 0 and r.b:
                    sum_states(r.s, t // 2 - 2)
                if r.d and t in (0, 1):
                    transpose_rows(r, t)
                if r.d and t == 2:
                    route(r)
                if r.a and 2 <= t <= 5:
                    for name in {2: ("in0",), 3: ("in1", "cv0"), 4: ("cv1", "in2"), 5: ("in3",)}[t]:
                        project(r, int(name[2])) if name[0] == "i" else convolve(r, int(name[2]))
                if r.d and t == 5:
                    count(r)
                if r.c and t in (6, 7):
                    project_out(r, t - 6)
                if r.a and t in (9, 10):
                    from_xc(r, f"dt{t - 9}", weight(DT_ + (t - 9) * P, P, w_hi), weight(DT_ + (t - 9) * P, P, w_lo))
                if r.a and t in (11, 12):
                    i = t - 11
                    from_xc(r, ("bb", "cc")[i], lambda k: bc_hi[:, k, i, :], lambda k: bc_lo[:, k, i, :])

    def act_stage1(act):
        act.wait_ge(s_const, SETUP)
        act.activation(rate[:, :], rate[:, :], ACT.Exp).then_inc(s_set_act, 1)
        act.wait_ge(s_set_dve, SET_DVE)

        def split_x(r):
            s = r.s.at(1)
            act.wait_ge(s_xt, 16 * (s.n + 1))
            act.activation(flat(xt_hi[:, :, :]), flat(xt[:, :, :]), ACT.Copy).then_inc(s_xt_hi, 1)

        def store_in(r, m):
            s = r.s.at(1)
            bank, done = full(act, r, f"in{m}")
            if m == 2:
                after(act, s_y, s.n - 1)
            to = xpad[:, m, TAPS - 1:TAPS - 1 + LEN] if m < 2 else sg[s.p][:, m - 2, :]
            act.activation(to, bank[:, :], ACT.Identity, bias=b_in[:, m:m + 1]).then_inc(done, 1)

        def store_conv(r, h):
            s = r.s.at(1)
            bank, done = full(act, r, f"cv{h}")
            after(act, s_skip, 2 * (s.n - 1))
            act.activation(xc[s.p][:, h, :], bank[:, :], ACT.Identity, bias=b_conv[:, h:h + 1]).then_inc(done, 1)

        def silu(r):
            s = r.s.at(1)
            for name in ("in3", "cv1"):
                bank, n = r.block(name)
                act.wait_ge(bank_read[bank], n)
            act.activation(flat(xc[s.p][:, :, :]), flat(xc[s.p][:, :, :]), ACT.Silu).then_inc(s_silu, 1)
            act.activation(flat(sg[s.p][:, :, :]), flat(sg[s.p][:, :, :]), ACT.Silu).then_inc(s_silu, 1)

        def split_xc(r):
            s = r.s.at(1)
            act.wait_ge(s_silu, 2 * s.n + 1)
            act.activation(flat(xc_hi[:, :, :]), flat(xc[s.p][:, :, :]), ACT.Copy).then_inc(s_xc_hi, 1)

        def store_dt(r, h):
            bank, done = full(act, r, f"dt{h}")
            if h == 0:
                after(act, s_lo, r.s.at(1).n)
            act.activation(relu[:, h, :], bank[:, :], ACT.Relu, bias=b_dt[:, h:h + 1])
            act.activation(expo[:, h, :], bank[:, :], ACT.Abs, bias=b_dt[:, h:h + 1]).then_inc(done, 1)

        def softplus(r):
            s = r.s.at(1)
            bank, n = r.block("dt1")
            act.wait_ge(bank_read[bank], n)
            act.activation(flat(expo[:, :, :]), flat(expo[:, :, :]), ACT.Exp, scale=-1.0).then_inc(s_exp, 1)
            act.wait_ge(s_exp, s.n + 1)
            if r.d:
                full(act, r, "rt")
            act.activation(flat(logp[:, :, :]), flat(expo[:, :, :]), ACT.Ln, bias=1.0).then_inc(s_log, 1)

        def store_bc(r, i):
            s = r.s.at(1)
            bank, done = full(act, r, ("bb", "cc")[i])
            after(act, s_read, SLOTS * (s.n - 1))
            to = (b_rep, c_rep)[i][s.p]
            act.activation(to[:, :], bank[:, :], ACT.Identity, bias=b_bc[:, i:i + 1]).then_inc(done, 1)

        def split_scan_inputs(r):
            s = r.s.at(1)
            act.wait_ge(s_dt, s.n + 1)
            act.wait_ge(s_u, s.n + 1)
            after(act, s_pu, SLOTS * (s.n - 1))
            for st, src in ((dt_st, expo), (u_st, relu)):
                act.activation(st[s.p][0:64, 0::2, :], src[0:64, :, :], ACT.Copy)
                last = act.activation(st[s.p][64:128, 1::2, :], src[64:128, :, :], ACT.Copy)
            last.then_inc(s_hi, 1)

        def decays(r, t):
            s = r.s
            quad, half, j, tiles = pair_of(t)
            after(act, s_state, SLOTS * s.n + t - 3)
            for i, c in enumerate(tiles):
                act.wait_ge(s_pdt, GROUPS * s.n + 2 * t + i + 1)
                g = 16 * half + j + 4 * c
                act.activation(decay[quad % 2][:, c, 1:LEN], p_dt[:, 1:LEN], ACT.Exp, scale=rate[:, g:g + 1])\
                   .then_inc(s_decay, 1)

        def split_y(r):
            s = r.s.at(-1)
            act.wait_ge(s_y, s.n + 1)
            after(act, s_x1, s.n)
            act.activation(flat(y_hi[:, :, :]), flat(y[:, :, :]), ACT.Copy).then_inc(s_y_hi, 1)

        def load_x(r):
            s = r.s
            after(act, s_norm, NORM_STEPS * (s.n - 1) + 5)
            act.dma_start(x[:, :, :], ins["x"][bass.ds(s.n, 1), :, :].rearrange("s (t p) d -> (s p) t d", p=P))\
               .then_inc(s_x, 16)

        def start_total(r):
            s = r.s.at(-1)
            act.wait_ge(s_x1, s.n + 1)
            act.dma_start(total_rows[bass.ds(s.n, 1), :, :, :].rearrange("s p t d -> (s p) t d"),
                          rows[s.p][:, :, 0:D]).then_inc(s_total[s.p], 16)

        def store_x1t(r, k):
            bank, done = full(act, r, f"tr{k}")
            act.wait_ge(s_sum, SEQS if not r.a else r.s.n + 1)
            act.activation(x1t[:, k, :], bank[:, :], ACT.Copy).then_inc(done, 1)

        def router_exp(r):
            s = r.s.at(-2)
            act.wait_ge(s_rexp, 2 * s.n + 1)
            act.activation(flat(ex[:, :, :]), flat(ex[:, :, :]), ACT.Exp).then_inc(s_rexp, 1)

        for r in rounds(act):
            for t in range(SLOTS):
                if r.b:
                    decays(r, t)
                if r.a and t == 0:
                    split_x(r)
                if r.d and t in (0, 1):
                    store_x1t(r, t)
                if r.a and 2 <= t <= 5:
                    for name in {2: ("in0",), 3: ("in1", "cv0"), 4: ("cv1", "in2"), 5: ("in3",)}[t]:
                        store_in(r, int(name[2])) if name[0] == "i" else store_conv(r, int(name[2]))
                if r.d and t == 4:
                    router_exp(r)
                if r.c and t == 5:
                    split_y(r)
                if r.a and t == 6:
                    silu(r)
                if r.a and t == 7:
                    split_xc(r)
                if r.a and t in (9, 10):
                    store_dt(r, t - 9)
                if r.a and t == 10:
                    softplus(r)
                if r.a and t in (11, 12):
                    store_bc(r, t - 11)
                if r.a and t == 13:
                    split_scan_inputs(r)
                if r.b and t == 13:
                    load_x(r)
                if r.c and t == 14:
                    start_total(r)

    SET_DVE = 3

    def dve_setup(dve):
        dve.wait_ge(s_const, SETUP)
        dve.memset(neg_half[:, :], -0.5)
        dve.tensor_copy(w_hi[:, 0, :], raw_w0)
        dve.tensor_copy(w_hi[:, 1, :], raw_w1)
        dve.tensor_copy(bo_hi[0:1, :], b_out)
        dve.tensor_copy(ones_r[:, :], c_ones)
        dve.tensor_copy(flat(pick[:, :, :]), raw_pick).then_inc(s_set_dve, 1)
        dve.wait_ge(s_set_dve, 1)
        dve.tensor_tensor(w_lo[:, 0, :], raw_w0, w_hi[:, 0, :].bitcast(F32), ALU.subtract)
        dve.tensor_tensor(w_lo[:, 1, :], raw_w1, w_hi[:, 1, :].bitcast(F32), ALU.subtract)
        dve.tensor_tensor(bo_lo[0:1, :], b_out, bo_hi[0:1, :].bitcast(F32), ALU.subtract)
        for i in range(HALVES * TAPS):
            dve.tensor_scalar(taps[:, i, :], ident[:, :], tap[:, i:i + 1], None, ALU.mult)
        for h in range(2):
            dve.memset(xpad[:, h, 0:TAPS - 1], 0.0)
            dve.memset(decay[h][:, :, 0:1], 0.0)
            dve.memset(rows[h][:, :, :], 0.0)
        dve.memset(chosen[:, :, :], 0.0)
        dve.tensor_copy(before[:, :], c_before)
        dve.tensor_copy(ones[:, :], c_ones).then_inc(s_set_dve, 1)
        dve.wait_ge(s_set_dve, 2)
        for k in range(KD):
            for part, to in ((w_hi, bc_hi), (w_lo, bc_lo)):
                for i in range(2):
                    src = part[:, k, BC + STATE * i:BC + STATE * (i + 1)].bitcast(F32)
                    dve.tensor_copy(to[:, k, i, :].rearrange("p (r n) -> p r n", n=STATE),
                                    src.unsqueeze(1).broadcast_to([P, CHPG, STATE]))
        dve.wait_ge(s_set_act, 1)
        dve.tensor_scalar(rate[:, :], rate[:, :], -1.0, None, ALU.mult).then_inc(s_set_dve, 1)

    def dve_stage1(dve):
        dve_setup(dve)

        def f32(ap):
            return ap.bitcast(F32)

        def split_x(r):
            s = r.s.at(1)
            dve.wait_ge(s_xt_hi, s.n + 1)
            after(dve, s_xc_hi, s.n)
            dve.tensor_tensor(flat(xt_lo[:, :, :]), flat(xt[:, :, :]), f32(flat(xt_hi[:, :, :])), ALU.subtract)\
               .then_inc(s_xt_lo, 1)

        def split_xc(r):
            s = r.s.at(1)
            dve.wait_ge(s_xc_hi, s.n + 1)
            dve.tensor_tensor(flat(xc_lo[:, :, :]), flat(xc[s.p][:, :, :]), f32(flat(xc_hi[:, :, :])), ALU.subtract)\
               .then_inc(s_xc_lo, 1)

        def softplus_rest(r):
            s = r.s.at(1)
            dve.wait_ge(s_exp, s.n + 1)
            dve.tensor_scalar(flat(rest[:, :, :]), flat(expo[:, :, :]), 1.0, -1.0, ALU.add, ALU.add).then_inc(s_rest0, 1)
            dve.wait_ge(s_log, s.n + 1)
            dve.tensor_tensor(flat(relu[:, :, :]), flat(relu[:, :, :]), flat(logp[:, :, :]), ALU.add).then_inc(s_sum, 1)

        def scan_inputs(r):
            s = r.s.at(1)
            dve.wait_ge(s_sum, s.n + 1)
            dve.wait_ge(s_rest, s.n + 1)
            dve.tensor_tensor(flat(expo[:, :, :]), flat(relu[:, :, :]), flat(rest[:, :, :]), ALU.add).then_inc(s_dt, 1)
            dve.wait_ge(s_dt, s.n + 1)
            dve.tensor_tensor(flat(relu[:, :, :]), flat(expo[:, :, :]), flat(xc[s.p][:, :, :]), ALU.mult).then_inc(s_u, 1)

        def split_scan_inputs(r):
            s = r.s.at(1)
            dve.wait_ge(s_hi, s.n + 1)
            for st, src in ((dt_st, expo), (u_st, relu)):
                dve.tensor_tensor(st[s.p][64:128, 0::2, :], src[0:64, :, :], f32(st[s.p][0:64, 0::2, :]), ALU.subtract)
                last = dve.tensor_tensor(st[s.p][0:64, 1::2, :], src[64:128, :, :], f32(st[s.p][64:128, 1::2, :]),
                                         ALU.subtract)
            last.then_inc(s_lo, 1)

        def weigh_inputs(r, t):
            s = r.s
            if t == 0:
                dve.wait_ge(s_hi, s.n + 1)
            dve.wait_ge(s_pu, SLOTS * s.n + t + 1)
            u = p_u[t % 2][:, :].rearrange("p (a b) -> p a b", a=2)
            dve.tensor_tensor(u, u, b_rep[s.p][:, :].unsqueeze(1).broadcast_to([P, 2, LEN]), ALU.mult).then_inc(s_bu, 1)

        def scan(s, t):
            quad, _, _, tiles = pair_of(t)
            n = SLOTS * s.n + t
            dve.wait_ge(s_bu, n + 1)
            dve.wait_ge(s_decay, 2 * n + 2)
            after(dve, s_read, n - 1)
            dve.tensor_tensor_scan(flat(state[t % 2][:, :, :]), flat(decay[quad % 2][:, tiles[0]:tiles[0] + 2, :]),
                                   p_u[t % 2][:, :], 0.0, ALU.mult, ALU.add).then_inc(s_state, 1)

        def skip_path(s, h):
            dve.wait_ge(s_quad, QUADS * s.n + 4 * h + 4)
            dve.scalar_tensor_tensor(y[:, h, :], xc[s.p][:, h, :], skip[:, h:h + 1], p_y[:, :], ALU.mult, ALU.add)\
               .then_inc(s_skip, 1)

        def gate(r):
            s = r.s.at(-1)
            dve.wait_ge(s_skip, 2 * s.n + 2)
            dve.tensor_tensor(flat(y[:, :, :]), flat(y[:, :, :]), flat(sg[s.p][:, :, :]), ALU.mult).then_inc(s_y, 1)

        def split_y(r):
            s = r.s.at(-1)
            dve.wait_ge(s_y_hi, s.n + 1)
            dve.tensor_tensor(flat(y_lo[:, :, :]), flat(y[:, :, :]), f32(flat(y_hi[:, :, :])), ALU.subtract)\
               .then_inc(s_y_lo, 1)

        def add_input(r, b):
            s = r.s.at(-1)
            bank, done = full(dve, r, f"o{b}")
            if b == 0:
                dve.wait_ge(s_x, 16 * (s.n + 1))
            dve.tensor_tensor(flat(z[:, 2 * b:2 * b + 2, :]), bank[:, :], flat(x[:, 2 * b:2 * b + 2, :]), ALU.add)\
               .then_inc(done, 1)

        def statistics(steps, which):
            for t in range(TT):
                last = dve.bn_stats(stats[:, which, t, :], z[:, t, :])
            steps.then(last)
            dve.memset(scrap[:, 0:1], 0.0)
            for t in range(TT):
                last = dve.bn_aggr(mv[:, which, t, :], stats[:, which, t, :])
            steps.then(last)
            steps.then(dve.tensor_scalar(mv[:, which, :, 1], mv[:, which, :, 1], EPS, None, ALU.add))

        def norm_start(r):
            s = r.s.at(-1)
            bank, n = r.block("o1")
            dve.wait_ge(bank_read[bank], n)
            bank, n = r.block("o0")
            dve.wait_ge(bank_read[bank], n)
            steps = Steps(dve, s_norm, s.n, NORM_STEPS)
            statistics(steps, 0)
            return steps

        def norm_apply(r, steps):
            s = r.s.at(-1)
            dve.wait_ge(s_rstd, 2 * s.n + 1)
            for t in range(TT):
                last = dve.tensor_scalar(z[:, t, :], z[:, t, :], mv[:, 0, t, 0:1], rstd[:, 0, t:t + 1],
                                         ALU.subtract, ALU.mult)
            steps.then(last)

        def residual(r, steps):
            s = r.s.at(-1)
            dve.wait_ge(s_scaled, s.n + 1)
            steps.then(dve.tensor_tensor(flat(z[:, :, :]), flat(z[:, :, :]), flat(x[:, :, :]), ALU.add))
            statistics(steps, 1)

        def second_norm(r, steps):
            s = r.s.at(-1)
            dve.wait_ge(s_rstd, 2 * s.n + 2)
            after(dve, s_scat[s.p], 16 * TT * TOPK * s.use)
            after(dve, s_total[s.p], 16 * s.use)
            for t in range(TT):
                last = dve.tensor_scalar(rows[s.p][:, t, 0:D], z[:, t, :], mv[:, 1, t, 0:1], rstd[:, 1, t:t + 1],
                                         ALU.subtract, ALU.mult)
            last.then_inc(s_x1, 1)
            assert steps.k == steps.per, steps.k

        def rank_experts(r):
            s = r.s.at(-2)
            bank, done = full(dve, r, "rt")
            steps = Steps(dve, s_route, s.n, ROUTE_STEPS)
            dve.tensor_tensor(lg[:, :, :], bank[:, 0:TT * E].rearrange("p (t e) -> p t e", e=E),
                              b_router[:, :].unsqueeze(1).broadcast_to([P, TT, E]), ALU.add).then_inc(done, 1)
            b, n = r.block("rt")
            dve.wait_ge(bank_read[b], n)
            other = lg[:, :, :].unsqueeze(2).broadcast_to([P, TT, E, E])
            own = lg[:, :, :].unsqueeze(3).broadcast_to([P, TT, E, E])
            dve.tensor_tensor(cmp[:, 0, :, :, :], other, own, ALU.is_ge)
            steps.then(dve.tensor_tensor(cmp[:, 1, :, :, :], other, own, ALU.is_gt))
            dve.tensor_tensor(cmp[:, 0, :, :, :], cmp[:, 0, :, :, :], lower[:, :, :].unsqueeze(1).broadcast_to([P, TT, E, E]), ALU.mult)
            steps.then(dve.tensor_tensor(cmp[:, 1, :, :, :], cmp[:, 1, :, :, :], upper[:, :, :].unsqueeze(1).broadcast_to([P, TT, E, E]), ALU.mult))
            steps.then(dve.tensor_tensor(cmp[:, 0, :, :, :], cmp[:, 0, :, :, :], cmp[:, 1, :, :, :], ALU.add))
            dve.tensor_reduce(top[:, :], lg[:, :, :], AX.X, ALU.max)
            steps.then(dve.tensor_reduce(rank[:, :, :], cmp[:, 0, :, :, :], AX.X, ALU.add))
            dve.tensor_scalar(chosen[:, 0:TT, :], rank[:, :, :], float(TOPK), None, ALU.is_lt).then_inc(s_chosen, 1)
            dve.tensor_tensor(ex[:, :, :], lg[:, :, :], top[:, :].unsqueeze(2).broadcast_to([P, TT, E]), ALU.subtract)\
               .then_inc(s_rexp, 1)
            return steps

        def weigh_experts(r, steps):
            s = r.s.at(-2)
            dve.wait_ge(s_rexp, 2 * s.n + 2)
            dve.wait_ge(s_chosen, s.n + 1)
            steps.then(dve.tensor_tensor(ex[:, :, :], ex[:, :, :], chosen[:, 0:TT, :], ALU.mult))
            steps.then(dve.tensor_reduce(den[:, 0, :], ex[:, :, :], AX.X, ALU.add))
            steps.then(dve.reciprocal(den[:, 1, :], den[:, 0, :]))
            dve.tensor_tensor(rows[s.p][:, :, COL_WEIGHT:COL_WEIGHT + E], ex[:, :, :],
                              den[:, 1, :].unsqueeze(2).broadcast_to([P, TT, E]), ALU.mult)
            steps.then(dve.tensor_copy(rows[s.p][:, :, COL_TOKEN].bitcast(I32), token[:, :]))
            steps.then(dve.tensor_scalar(token[:, :], token[:, :], float(LEN), None, ALU.add))

        def places(r, steps):
            s = r.s.at(-2)
            bank, done = full(dve, r, "cnt")
            steps.then(dve.tensor_tensor(place[:, :, :], bank[:, 0:TT * E].rearrange("p (t e) -> p t e", e=E),
                                         base[:, :].unsqueeze(1).broadcast_to([P, TT, E]), ALU.add))
            dve.tensor_tensor(base[:, :], base[:, :], bank[:, TT * E:(TT + 1) * E], ALU.add).then_inc(done, 1)
            steps.then(dve.tensor_tensor(spot[:, :, :, :], rank[:, :, :].unsqueeze(2).broadcast_to([P, TT, TOPK, E]),
                                         slot[:, :, :].unsqueeze(1).broadcast_to([P, TT, TOPK, E]), ALU.is_equal))
            steps.then(dve.tensor_tensor(spot[:, :, :, :], spot[:, :, :, :],
                                         place[:, :, :].unsqueeze(2).broadcast_to([P, TT, TOPK, E]), ALU.mult))
            steps.then(dve.tensor_reduce(spot_sum[:, :, :], spot[:, :, :, :], AX.X, ALU.add))
            assert steps.k == steps.per, steps.k
            dve.tensor_copy(index[s.p][:, :], flat(spot_sum[:, :, :])).then_inc(s_index, 1)

        for r in rounds(dve):
            for t in range(SLOTS):
                if r.b:
                    weigh_inputs(r, t)
                if t == 0 and r.c:
                    scan(r.s.at(-1), SLOTS - 1)
                if t > 0 and r.b:
                    scan(r.s, t - 1)
                if r.a and t == 0:
                    split_x(r)
                if r.d and t == 3:
                    route_steps = rank_experts(r)
                if r.c and t == 3:
                    skip_path(r.s.at(-1), 1)
                if r.c and t == 4:
                    gate(r)
                if r.c and t == 5:
                    split_y(r)
                if r.d and t == 5:
                    weigh_experts(r, route_steps)
                if r.c and t in (7, 8):
                    add_input(r, t - 7)
                if r.a and t == 8:
                    split_xc(r)
                if r.c and t == 8:
                    norm_steps = norm_start(r)
                if r.c and t == 9:
                    norm_apply(r, norm_steps)
                if r.d and t == 6:
                    places(r, route_steps)
                if r.b and t == 11:
                    skip_path(r.s, 0)
                if r.c and t == 11:
                    residual(r, norm_steps)
                if r.a and t == 11:
                    softplus_rest(r)
                if r.c and t == 12:
                    second_norm(r, norm_steps)
                if r.a and t == 12:
                    scan_inputs(r)
                if r.a and t == 14:
                    split_scan_inputs(r)

    def pool_stage1(pool):
        pool.wait_ge(s_set_dve, SET_DVE)

        def read_state(s, t):
            quad, _, _, tiles = pair_of(t)
            n = SLOTS * s.n + t
            pool.wait_ge(s_state, n + 1)
            after(pool, s_quad, QUADS * s.n + quad - 1)
            pool.tensor_tensor(read[quad % 2][:, tiles[0]:tiles[0] + 2, :], state[t % 2][:, :, :],
                               c_rep[s.p][:, :].unsqueeze(1).broadcast_to([P, 2, LEN]), ALU.mult).then_inc(s_read, 1)

        def power(s, which):
            pool.wait_ge(s_norm, NORM_STEPS * s.n + (3 if which == 0 else 8))
            pool.tensor_tensor(rstd[:, which, :], mv[:, which, :, 1], neg_half[:, :], ALU.pow).then_inc(s_rstd, 1)

        def scale(r):
            s = r.s.at(-1)
            pool.tensor_tensor(x[:, :, :], x[:, :, :], ln_b[:, :].unsqueeze(1).broadcast_to([P, TT, D]), ALU.add)
            pool.wait_ge(s_norm, NORM_STEPS * s.n + 4)
            pool.tensor_tensor(z[:, :, :], z[:, :, :], ln_g[:, :].unsqueeze(1).broadcast_to([P, TT, D]), ALU.mult)\
                .then_inc(s_scaled, 1)

        def softplus_rest(r):
            s = r.s.at(1)
            pool.wait_ge(s_rest0, s.n + 1)
            pool.tensor_tensor(rest[:, :, :], expo[:, :, :], rest[:, :, :], ALU.subtract).then_inc(s_rest, 1)

        def scatter(r, some):
            s = r.s.at(-2)
            if 0 in some:
                pool.wait_ge(s_index, s.n + 1)
                after(pool, s_scrap, s.n)
                pool.tensor_tensor(scrap[:, 1:2], neg_half[:, 0:1], neg_half[:, 0:1], ALU.mult).then_inc(s_scrap, 1)
            for i in some:
                pool.indirect_dma_start(queues, bass.IndirectOffsetOnAxis(ap=index[s.p][:, i:i + 1], axis=0),
                                        rows[s.p][:, i // TOPK, :], None).then_inc(s_scat[s.p], 16)

        for r in rounds(pool):
            for t in range(SLOTS):
                if t == 0 and r.c:
                    read_state(r.s.at(-1), SLOTS - 1)
                if t > 0 and r.b:
                    read_state(r.s, t - 1)
                if r.c and t == 8:
                    power(r.s.at(-1), 0)
                if r.c and t == 9:
                    scale(r)
                if r.c and t == 11:
                    power(r.s.at(-1), 1)
                if r.a and t == 11:
                    softplus_rest(r)
                if r.d and t >= 12:
                    scatter(r, range(4 * (t - 12), 4 * (t - 12) + 4))

    def sp_stage1(sp):
        for to, src in loads:
            sp.dma_start(to, src).then_inc(s_const, 16)

        def load_sequence(s):
            after(sp, s_xt_lo, s.n)
            sp.dma_start(xt[:, :, :], ins["x_t"][bass.ds(s.n, 1), :, :].rearrange("s (k p) l -> (s p) k l", p=P))\
              .then_inc(s_xt, 16)

        for s in range(2):
            load_sequence(Seq(0, s))
        with sp.Fori(1, SEQS // 2) as half:
            for s in range(2):
                load_sequence(Seq(half, s))

    with nc.Block() as block:
        @block.tensor
        def _(pe):
            pe_stage1(pe)

        @block.scalar
        def _(act):
            act_stage1(act)

        @block.vector
        def _(dve):
            dve_stage1(dve)

        @block.gpsimd
        def _(pool):
            pool_stage1(pool)

        @block.sync
        def _(sp):
            sp_stage1(sp)
            for i in range(2):
                sp.wait_ge(s_total[i], 16 * (SEQS // 2))
                sp.wait_ge(s_scat[i], 16 * TT * TOPK * (SEQS // 2))

    pone.close()
    one.close()
    two = ctx.enter_context(ExitStack())
    ptwo = ctx.enter_context(ExitStack())
    GU = KD * 2 * INNER
    NWE = GU + CH * D
    c_tile = sb("c_tile", PLANNED, E, at=two)
    one_row = sb("one_row", E, at=two)
    used = sb("used", E, at=two)
    used_i = sb("used_i", E, dt=I32, at=two)
    tiles_e = sb("tiles_e", E, at=two)
    upto = sb("upto", E, at=two)
    first = sb("first", E, at=two)
    past = sb("past", 2, PLANNED, E, at=two)
    t_expert = sb("t_expert", PLANNED, at=two)
    t_start = sb("t_start", PLANNED, at=two)
    t_row = sb("t_row", PLANNED, at=two)
    t_valid = sb("t_valid", PLANNED, at=two)
    expert_i = sb("expert_i", PLANNED, dt=I32, at=two)
    row_i = sb("row_i", PLANNED, dt=I32, at=two)
    base_i = sb("base_i", E, dt=I32, at=two)
    pairs_f = sb("pairs_f", 1, at=two)
    pairs_i = sb("pairs_i", 1, dt=I32, at=two)
    pad = sb("pad", SUBS, ROW, at=two)

    raw_w = [sb(f"raw_w{i}", W_ALL, at=two) for i in range(2)]
    wh = [sb(f"wh{i}", NWE, dt=F32R, at=two) for i in range(2)]
    wl = [sb(f"wl{i}", NWE, dt=F32R, at=two) for i in range(2)]
    bias = [sb(f"bias{i}", 2, CH, at=two) for i in range(2)]
    b_down = [sb(f"b_down{i}", D, at=two) for i in range(2)]
    xq = [sb(f"xq{i}", SUBS, ROW, at=two) for i in range(2)]
    tok = [sb(f"tok{i}", SUBS, dt=U32, at=two) for i in range(2)]
    share = [sb(f"share{i}", SUBS, at=two) for i in range(2)]
    xh = [sb(f"xh{i}", KD, TILE, dt=F32R, at=two) for i in range(2)]
    xl = [sb(f"xl{i}", KD, TILE, dt=F32R, at=two) for i in range(2)]
    gate_v = [sb(f"gate_v{i}", TILE, at=two) for i in range(2)]
    up_v = [sb(f"up_v{i}", TILE, at=two) for i in range(2)]
    sig = [sb(f"sig{i}", TILE, at=two) for i in range(2)]
    a_v = [sb(f"a_v{i}", TILE, at=two) for i in range(2)]
    ah = sb("ah", CH, TILE, dt=F32R, at=two)
    al = sb("al", CH, TILE, dt=F32R, at=two)
    o_v = [sb(f"o_v{i}", SUBS, D, at=two) for i in range(2)]

    p_x = [ps(f"p_x{i}", TILE, at=ptwo) for i in range(KD)]
    p_g = [ps(f"p_g{i}", TILE, at=ptwo) for i in range(2)]
    p_up = [ps(f"p_up{i}", TILE, at=ptwo) for i in range(2)]
    p_o = [ps(f"p_o{i}", 2 * D, at=ptwo) for i in range(2)]

    s_scrap2 = sem("s_scrap2")
    s_tload, s_plan, s_tables, s_pad = sem("s_tload"), sem("s_plan"), sem("s_tables"), sem("s_pad")
    s_w = [sem(f"s_w{i}") for i in range(2)]
    s_rows = [sem(f"s_rows{i}") for i in range(2)]
    s_wh, s_wl, s_bias = sem("s_wh"), sem("s_wl"), sem("s_bias")
    s_tr, s_xh, s_xl = sem("s_tr"), sem("s_xh"), sem("s_xl")
    s_gu, s_g, s_up, s_prod, s_sig, s_a, s_ah, s_al = (sem(n) for n in ("s_gu", "s_g", "s_up", "s_prod", "s_sig", "s_a", "s_ah", "s_al"))
    s_down, s_o, s_scaled_o, s_tok, s_share = (sem(n) for n in ("s_down", "s_o", "s_scaled_o", "s_tok", "s_share"))
    s_add = [sem(f"s_add{i}") for i in range(2)]
    ADDS = 16 * SUBS
    LAG = 2

    def plan(dve):
        dve.wait_ge(s_tload, 16)
        steps = Steps(dve, s_plan, 0, 15)
        dve.memset(one_row[:, :], 1.0)
        dve.memset(pad[:, :, :], 0.0)
        dve.tensor_copy(base_i[:, :], base[:, :])
        steps.then(dve.tensor_tensor(used[:, :], base[:, :], c_queue[:, :], ALU.subtract))
        dve.tensor_copy(pad[:, :, COL_TOKEN].bitcast(I32), c_spill[:, :])
        steps.then(dve.tensor_scalar(used_i[:, :], used[:, :], float(TILE - 1), None, ALU.add))
        steps.then(dve.tensor_scalar(used_i[:, :], used_i[:, :], TILE.bit_length() - 1, None, ALU.arith_shift_right))
        steps.then(dve.tensor_copy(tiles_e[:, :], used_i[:, :]))
        steps.then(dve.tensor_tensor_scan(upto[:, :], one_row[:, :], tiles_e[:, :], 0.0, ALU.mult, ALU.add))
        steps.then(dve.tensor_tensor(first[:, :], upto[:, :], tiles_e[:, :], ALU.subtract))
        dve.tensor_scalar(t_valid[:, :], c_tile[:, :, 0], upto[:, E - 1:E], None, ALU.is_lt)
        dve.tensor_scalar(pairs_f[:, :], upto[:, E - 1:E], -1.0, None, ALU.add)
        for i, edge in enumerate((upto, first)):
            last = dve.tensor_tensor(past[:, i, :, :], edge[:, :].unsqueeze(1).broadcast_to([P, PLANNED, E]),
                                     c_tile[:, :, :], ALU.is_le)
        steps.then(last)
        dve.tensor_copy(pairs_i[:, :], pairs_f[:, :])
        dve.tensor_reduce(t_expert[:, :], past[:, 0, :, :], AX.X, ALU.add)
        steps.then(dve.tensor_tensor(past[:, 1, :, :], past[:, 1, :, :],
                                     first[:, :].unsqueeze(1).broadcast_to([P, PLANNED, E]), ALU.mult))
        dve.tensor_scalar(pairs_i[:, :], pairs_i[:, :], 1, None, ALU.arith_shift_right)
        dve.tensor_scalar(t_expert[:, :], t_expert[:, :], float(E - 1), None, ALU.min)
        steps.then(dve.tensor_reduce(t_start[:, :], past[:, 1, :, :], AX.X, ALU.max))
        dve.tensor_copy(expert_i[:, :], t_expert[:, :])
        dve.tensor_scalar(t_expert[:, :], t_expert[:, :], float(QUEUE), float(-E * QUEUE), ALU.mult, ALU.add)
        steps.then(dve.tensor_tensor(t_row[:, :], c_tile[:, :, 0], t_start[:, :], ALU.subtract))
        steps.then(dve.tensor_scalar(t_row[:, :], t_row[:, :], float(TILE), None, ALU.mult))
        steps.then(dve.tensor_tensor(t_row[:, :], t_row[:, :], t_expert[:, :], ALU.add))
        steps.then(dve.tensor_tensor(t_row[:, :], t_row[:, :], t_valid[:, :], ALU.mult))
        steps.then(dve.tensor_scalar(t_row[:, :], t_row[:, :], float(E * QUEUE), None, ALU.add))
        steps.then(dve.tensor_copy(row_i[:, :], t_row[:, :]))
        assert steps.k == steps.per, steps.k
        dve.memset(scrap[:, 0:1], 0.0).then_inc(s_tables, 1)

    def last_pair(eng):
        return eng.value_load(pairs_i[0:1, 0:1], min_val=TOKENS * TOPK // TILE // 2 - 1, max_val=TILES // 2 - 1)

    def tiles(eng, last_p):
        for k in range(2):
            yield Seq(0, k)
        with eng.Fori(1, last_p + 1) as pair:
            for k in range(2):
                yield Seq(pair, k)

    def pe_stage2(pe):
        pe.wait_ge(s_tables, 1)
        last_p = last_pair(pe)

        def transpose_tile(t):
            pe.wait_ge(s_rows[t.p], 16 * (t.use + 1))
            after(pe, s_xl, KD * t.n)
            for k in range(KD):
                for a in range(SUBS):
                    mm = pe.transpose(p_x[k][:, a * P:(a + 1) * P], xq[t.p][:, a, k * P:(k + 1) * P], ident[:, :])
                mm.then_inc(s_tr, 1)

        def up_projection(t, i):
            n = CH * t.n + i
            if i == 0:
                pe.wait_ge(s_xl, KD * (t.n + 1))
                pe.wait_ge(s_wl, 2 * t.n + 1)
            after(pe, s_up, n - 1)
            for to, at in ((p_g[i % 2], i * P), (p_up[i % 2], INNER + i * P)):
                for k in range(KD):
                    c = k * 2 * INNER + at
                    for m, (w, v) in enumerate(((wh, xh), (wh, xl), (wl, xh))):
                        mm = pe.matmul(to[:, :], w[t.p][:, c:c + P], v[t.p][:, k, :],
                                       start=(k == 0 and m == 0), stop=(k == KD - 1 and m == 2))
            mm.then_inc(s_gu, 1)

        def down_projection(t, i):
            n = CH * t.n + i
            if i == 0:
                pe.wait_ge(s_wl, 2 * t.n + 2)
                after(pe, s_o, 2 * t.n)
            pe.wait_ge(s_ah, n + 1)
            pe.wait_ge(s_al, n + 1)
            c = GU + i * D
            for a in range(SUBS):
                to = p_o[a // 2][:, (a % 2) * D:(a % 2 + 1) * D]
                for m, (v, w) in enumerate(((ah, wh), (ah, wl), (al, wh))):
                    mm = pe.matmul(to, v[:, i, a * P:(a + 1) * P], w[t.p][:, c:c + D],
                                   start=(i == 0 and a % 2 == 0 and m == 0), stop=(i == CH - 1 and m == 2),
                                   skip_group_check=True)
            mm.then_inc(s_down, 1)

        transpose_tile(Seq(0, 0))
        for t in tiles(pe, last_p):
            for i in range(CH):
                up_projection(t, i)
                if i == 2:
                    transpose_tile(t.at(1))
                if i >= LAG:
                    down_projection(t, i - LAG)
                elif t.off > 0 or not isinstance(t.half, int):
                    down_projection(t.at(-1), i + CH - LAG)
        end = Seq(last_p, 1)
        for i in range(LAG):
            down_projection(end, i + CH - LAG)

    def act_stage2(act):
        act.wait_ge(s_tables, 1)
        last_p = last_pair(act)

        def copy_weights(t, part):
            if part == 0:
                act.wait_ge(s_w[t.p], 16 * (t.use + 1))
                after(act, s_gu, CH * (t.n - 1))
            if part == 2:
                after(act, s_down, CH * (t.n - 1))
            at = slice(part * GU // 2, (part + 1) * GU // 2) if part < 2 else slice(GU, NWE)
            act.activation(wh[t.p][:, at], raw_w[t.p][:, at], ACT.Copy).then_inc(s_wh, 1)

        def copy_tile(t, k):
            act.wait_ge(s_tr, KD * t.n + k + 1)
            if k == 0:
                after(act, s_gu, CH * (t.n - 1))
            act.activation(xh[t.p][:, k, :], p_x[k][:, :], ACT.Copy).then_inc(s_xh, 1)

        def sigmoid(t, i):
            n = CH * t.n + i
            act.wait_ge(s_g, n + 1)
            after(act, s_a, n - 1)
            act.activation(sig[i % 2][:, :], gate_v[i % 2][:, :], ACT.Sigmoid, scale=ALPHA).then_inc(s_sig, 1)

        def copy_product(t, i):
            n = CH * t.n + i
            act.wait_ge(s_a, n + 1)
            after(act, s_down, n - CH + 1)
            act.activation(ah[:, i, :], a_v[i % 2][:, :], ACT.Copy).then_inc(s_ah, 1)

        def copy_share(t, expert):
            act.wait_ge(s_rows[t.p], 16 * (t.use + 1))
            act.activation(share[t.p][:, :], xq[t.p][:, :, bass.ds(expert + COL_WEIGHT, 1)].rearrange("p a b -> p (a b)"),
                           ACT.Copy).then_inc(s_share, 1)

        def weigh_output(t):
            act.wait_ge(s_share, t.n + 1)
            for a in range(SUBS):
                if a % 2 == 0:
                    act.wait_ge(s_o, 2 * t.n + a // 2 + 1)
                last = act.activation(o_v[t.p][:, a, :], o_v[t.p][:, a, :], ACT.Copy, scale=share[t.p][:, a:a + 1])
            last.then_inc(s_scaled_o, 1)

        first_tile = Seq(0, 0)
        for k in range(KD):
            copy_tile(first_tile, k)
        for part in range(3):
            copy_weights(first_tile, part)
        for t in tiles(act, last_p):
            later = t.off > 0 or not isinstance(t.half, int)
            expert = act.value_load(expert_i[0:1, bass.ds(t.n, 1)], min_val=0, max_val=E - 1)
            for i in range(CH):
                if i > 0:
                    copy_product(t, i - 1)
                elif later:
                    copy_product(t.at(-1), CH - 1)
                sigmoid(t, i)
                if i == 0:
                    copy_share(t, expert)
                if i < 2:
                    copy_weights(t.at(1), i)
                if i == 2 and later:
                    weigh_output(t.at(-1))
                if i == 3:
                    for k in range(KD):
                        copy_tile(t.at(1), k)
                    copy_weights(t.at(1), 2)
        end = Seq(last_p, 1)
        copy_product(end, CH - 1)
        weigh_output(end)

    def dve_stage2(dve):
        plan(dve)
        last_p = last_pair(dve)

        def read_bias(t):
            dve.wait_ge(s_w[t.p], 16 * (t.use + 1))
            dve.tensor_copy(bias[t.p][:, 0, :], raw_w[t.p][:, NWE:NWE + CH])
            dve.tensor_scalar(bias[t.p][:, 1, :], raw_w[t.p][:, NWE + CH:NWE + 2 * CH], 1.0, None, ALU.add)
            dve.tensor_copy(b_down[t.p][:, :], raw_w[t.p][:, NWE + 2 * CH:W_ALL]).then_inc(s_bias, 1)

        def rest_of_tile(t, k):
            dve.wait_ge(s_xh, KD * t.n + k + 1)
            dve.tensor_tensor(xl[t.p][:, k, :], p_x[k][:, :], xh[t.p][:, k, :].bitcast(F32), ALU.subtract)\
               .then_inc(s_xl, 1)

        def read_chunk(t, i):
            n = CH * t.n + i
            dve.wait_ge(s_gu, n + 1)
            if i == 0:
                dve.wait_ge(s_bias, t.n + 1)
            dve.tensor_scalar(gate_v[i % 2][:, :], p_g[i % 2][:, :], bias[t.p][:, 0, i:i + 1], LIMIT, ALU.add, ALU.min)\
               .then_inc(s_g, 1)
            dve.tensor_scalar(up_v[i % 2][:, :], p_up[i % 2][:, :], bias[t.p][:, 1, i:i + 1], LIMIT + 1.0,
                              ALU.add, ALU.min).then_inc(s_up, 1)

        def rest_of_product(t, i):
            n = CH * t.n + i
            dve.wait_ge(s_ah, n + 1)
            dve.tensor_tensor(al[:, i, :], a_v[i % 2][:, :], ah[:, i, :].bitcast(F32), ALU.subtract).then_inc(s_al, 1)

        def product_of_chunk(t, i):
            n = CH * t.n + i
            dve.wait_ge(s_up, n + 1)
            dve.scalar_tensor_tensor(up_v[i % 2][:, :], up_v[i % 2][:, :], 1.0 - LIMIT, gate_v[i % 2][:, :],
                                     ALU.max, ALU.mult).then_inc(s_prod, 1)
            dve.wait_ge(s_prod, n + 1)
            dve.wait_ge(s_sig, n + 1)
            dve.tensor_tensor(a_v[i % 2][:, :], up_v[i % 2][:, :], sig[i % 2][:, :], ALU.mult).then_inc(s_a, 1)

        def copy_tokens(t):
            dve.wait_ge(s_rows[t.p], 16 * (t.use + 1))
            after(dve, s_add[t.p], ADDS * t.use)
            dve.tensor_copy(tok[t.p][:, :], xq[t.p][:, :, COL_TOKEN].bitcast(I32)).then_inc(s_tok, 1)

        def read_output(t):
            for b in range(2):
                if b == 0:
                    dve.wait_ge(s_down, CH * (t.n + 1))
                dve.tensor_tensor(o_v[t.p][:, 2 * b:2 * b + 2, :], p_o[b][:, :].rearrange("p (a d) -> p a d", d=D),
                                  b_down[t.p][:, :].unsqueeze(1).broadcast_to([P, 2, D]), ALU.add).then_inc(s_o, 1)

        for k in range(KD):
            rest_of_tile(Seq(0, 0), k)
        read_bias(Seq(0, 0))
        for t in tiles(dve, last_p):
            later = t.off > 0 or not isinstance(t.half, int)
            for i in range(CH):
                read_chunk(t, i)
                if i > 0:
                    rest_of_product(t, i - 1)
                elif later:
                    rest_of_product(t.at(-1), CH - 1)
                product_of_chunk(t, i)
                if i == 0:
                    copy_tokens(t)
                if i == 1 and later:
                    read_output(t.at(-1))
                if i == 2:
                    read_bias(t.at(1))
                if i == 3:
                    for k in range(KD):
                        rest_of_tile(t.at(1), k)
        end = Seq(last_p, 1)
        rest_of_product(end, CH - 1)
        read_output(end)

    def pool_stage2(pool):
        pool.wait_ge(s_tables, 1)
        last_p = last_pair(pool)

        def rest_of_weights(t, part):
            pool.wait_ge(s_wh, 3 * t.n + 2 + part)
            at = slice(0, GU) if part == 0 else slice(GU, NWE)
            pool.tensor_tensor(wl[t.p][:, at], raw_w[t.p][:, at], wh[t.p][:, at].bitcast(F32), ALU.subtract)\
                .then_inc(s_wl, 1)

        def add_output(t):
            if t.off != 0 or not isinstance(t.half, int):
                last = t.at(-1)
                pool.wait_ge(s_add[last.p], ADDS * (last.use + 1))
            pool.wait_ge(s_tok, t.n + 1)
            pool.wait_ge(s_scaled_o, t.n + 1)
            after(pool, s_scrap2, t.n)
            pool.tensor_tensor(scrap[:, 1:2], neg_half[:, 0:1], neg_half[:, 0:1], ALU.mult).then_inc(s_scrap2, 1)
            for a in range(SUBS):
                pool.indirect_dma_start(total, bass.IndirectOffsetOnAxis(ap=tok[t.p][:, a:a + 1], axis=0),
                                        o_v[t.p][:, a, :], None, compute_op=ALU.add).then_inc(s_add[t.p], 16)

        for part in range(2):
            rest_of_weights(Seq(0, 0), part)
        pool.wait_ge(s_pad, 16 * (E + 2))
        for t in tiles(pool, last_p):
            rest_of_weights(t.at(1), 0)
            if t.off > 0 or not isinstance(t.half, int):
                add_output(t.at(-1))
            rest_of_weights(t.at(1), 1)
        add_output(Seq(last_p, 1))

    def sp_stage2(sp):
        sp.dma_start(flat(c_tile[:, :, :]), ins["tile"]).then_inc(s_tload, 16)
        sp.wait_ge(s_tables, 1)
        last_p = last_pair(sp)
        for e in range(E):
            row = sp.value_load(base_i[0:1, e:e + 1], min_val=e * QUEUE, max_val=e * QUEUE + TOKENS)
            sp.dma_start(queues[bass.ds(row, TILE), :].rearrange("(p a) c -> p a c", a=SUBS), pad[:, :, :]).then_inc(s_pad, 16)
        sp.dma_start(queues[E * QUEUE:, :].rearrange("(p a) c -> p a c", a=SUBS), pad[:, :, :]).then_inc(s_pad, 16)
        sp.dma_start(total[TOKENS:, :].rearrange("(p a) d -> p a d", a=SUBS), pad[:, :, 0:D]).then_inc(s_pad, 16)

        def load_weights(t):
            expert = sp.value_load(expert_i[0:1, bass.ds(t.n, 1)], min_val=0, max_val=E - 1)
            after(sp, s_wl, 2 * (t.n - 1))
            after(sp, s_bias, t.n - 1)
            sp.dma_start(raw_w[t.p][:, :], ins["w_experts"][bass.ds(expert, 1), :, :].rearrange("e p c -> (e p) c"))\
              .then_inc(s_w[t.p], 16)

        def load_rows(t):
            row = sp.value_load(row_i[0:1, bass.ds(t.n, 1)], min_val=0, max_val=E * QUEUE)
            after(sp, s_tok, t.n - 1)
            after(sp, s_share, t.n - 1)
            after(sp, s_tr, KD * (t.n - 1))
            sp.dma_start(xq[t.p][:, :, :], queues[bass.ds(row, TILE), :].rearrange("(p a) c -> p a c", a=SUBS))\
              .then_inc(s_rows[t.p], 16)

        load_weights(Seq(0, 0))
        sp.wait_ge(s_pad, 16 * (E + 2))
        load_rows(Seq(0, 0))
        for t in tiles(sp, last_p):
            load_weights(t.at(1))
            load_rows(t.at(1))
        return last_p

    stage2_ends = []

    with nc.Block() as block:
        @block.tensor
        def _(pe):
            pe_stage2(pe)

        @block.scalar
        def _(act):
            act_stage2(act)

        @block.vector
        def _(dve):
            dve_stage2(dve)

        @block.gpsimd
        def _(pool):
            pool_stage2(pool)

        @block.sync
        def _(sp):
            last_p = sp_stage2(sp)
            waits = [(s_w[0], 16 * (last_p + 2)), (s_rows[0], 16 * (last_p + 2))]
            waits += [(s_add[i], ADDS * (last_p + 1)) for i in range(2)]
            stage2_ends.extend(waits)

    ptwo.close()
    two.close()
    three = ctx.enter_context(ExitStack())
    sums = [sb(f"sums{i}", TT, D, at=three) for i in range(2)]
    normed = [sb(f"normed{i}", TT, D, at=three) for i in range(2)]
    stats3 = [sb(f"stats3_{i}", TT, 6, at=three) for i in range(2)]
    mv3 = [sb(f"mv3_{i}", TT, 2, at=three) for i in range(2)]
    rstd3 = [sb(f"rstd3_{i}", TT, at=three) for i in range(2)]
    s_sums = [sem(f"s_sums{i}") for i in range(2)]
    s_store = [sem(f"s_store{i}") for i in range(2)]
    s_stats3, s_rstd3, s_normed = sem("s_stats3"), sem("s_rstd3"), sem("s_normed")

    def sequences(eng):
        for s in range(2):
            yield Seq(0, s)
        with eng.Fori(1, SEQS // 2) as half:
            for s in range(2):
                yield Seq(half, s)

    with nc.Block() as block:
        @block.sync
        def _(sp):
            for s_done, n in stage2_ends:
                sp.wait_ge(s_done, n)
            for s in sequences(sp):
                after(sp, s_normed, s.n - 1)
                sp.dma_start(sums[s.p][:, :, :], total_rows[bass.ds(s.n, 1), :, :, :].rearrange("s p t d -> (s p) t d"))\
                  .then_inc(s_sums[s.p], 16)

        @block.vector
        def _(dve):
            def statistics3(s):
                steps = Steps(dve, s_stats3, s.n, 3)
                dve.wait_ge(s_sums[s.p], 16 * (s.use + 1))
                for t in range(TT):
                    last = dve.bn_stats(stats3[s.p][:, t, :], sums[s.p][:, t, :])
                steps.then(last)
                dve.memset(scrap[:, 0:1], 0.0)
                for t in range(TT):
                    last = dve.bn_aggr(mv3[s.p][:, t, :], stats3[s.p][:, t, :])
                steps.then(last)
                steps.last(dve.tensor_scalar(mv3[s.p][:, :, 1], mv3[s.p][:, :, 1], EPS, None, ALU.add))

            def normalise3(s):
                dve.wait_ge(s_rstd3, s.n + 1)
                after(dve, s_store[s.p], 16 * s.use)
                for t in range(TT):
                    last = dve.tensor_scalar(normed[s.p][:, t, :], sums[s.p][:, t, :], mv3[s.p][:, t, 0:1],
                                             rstd3[s.p][:, t:t + 1], ALU.subtract, ALU.mult)
                last.then_inc(s_normed, 1)

            for s in sequences(dve):
                statistics3(s)
                normalise3(s)

        @block.gpsimd
        def _(pool):
            for s in sequences(pool):
                pool.wait_ge(s_stats3, 3 * (s.n + 1))
                pool.tensor_tensor(rstd3[s.p][:, :], mv3[s.p][:, :, 1], neg_half[:, :], ALU.pow).then_inc(s_rstd3, 1)

        @block.scalar
        def _(act):
            for s in sequences(act):
                act.wait_ge(s_normed, s.n + 1)
                act.dma_start(out_rows[bass.ds(s.n, 1), :, :, :].rearrange("s p t d -> (s p) t d"), normed[s.p][:, :, :])\
                   .then_inc(s_store[s.p], 16)
            for i in range(2):
                act.wait_ge(s_store[i], 16 * (SEQS // 2))


def kernel(**inputs):
    import concourse.bacc as bacc
    from concourse.bass_utils import run_bass_kernel_spmd

    i = {k.split("_", 2)[2] if k.startswith("L0_attn") else k[3:]: np.asarray(v) for k, v in inputs.items()}
    x = np.ascontiguousarray(i["x"])

    def cols(v):
        return np.ascontiguousarray(v.reshape(-1, P).T)

    arrays = {
        "x": x,
        "x_t": np.ascontiguousarray(x.transpose(0, 2, 1)),
        "w_in_t": np.ascontiguousarray(i["in_proj_w"].T),
        "w_dt_t": np.ascontiguousarray(i["dt_w"].T),
        "w_out_t": np.ascontiguousarray(i["out_w"].T),
        "w_bc_t": np.ascontiguousarray(i["bc_w"].T),
        "w_router_t": np.ascontiguousarray(i["ffn_router_weight"].T),
        "a_log_rows": np.ascontiguousarray(i["A_log"].reshape(GROUPS, P).T),
        "b_in": cols(i["in_proj_b"]),
        "b_conv": cols(i["conv_b"]),
        "b_dt": cols(i["dt_b"]),
        "skip": cols(i["D"]),
        "b_bc_rows": np.ascontiguousarray(np.tile(i["bc_b"].reshape(2, STATE), (1, CHPG)).T),
        "taps": np.ascontiguousarray(i["conv_w"].reshape(HALVES, P, TAPS).transpose(1, 0, 2).reshape(P, -1)),
        "b_out": i["out_b"].reshape(1, D),
        "ln_g": i["ln_g"],
        "ln_b": i["ln_b"],
        "b_router": i["ffn_router_bias"],
        "w_experts": np.concatenate([
            i["ffn_gate_up_proj"].reshape(E, 2 * INNER, KD, P).transpose(0, 3, 2, 1).reshape(E, P, -1),
            i["ffn_down_proj"].reshape(E, D, CH, P).transpose(0, 3, 2, 1).reshape(E, P, -1),
            i["ffn_gate_up_proj_bias"].reshape(E, 2 * CH, P).transpose(0, 2, 1),
            np.broadcast_to(i["ffn_down_proj_bias"][:, None, :], (E, P, D))], axis=2),
        **CONSTANTS,
    }
    nc = bacc.Bacc("TRN2", target_bir_lowering=False, num_devices=1)
    ins = {k: nc.dram_tensor(f"in_{k}", a.shape, mybir.dt.from_np(a.dtype), kind="ExternalInput").ap()
           for k, a in arrays.items()}
    out = nc.dram_tensor("out", (SEQS, LEN, D), F32, kind="ExternalOutput").ap()
    program(nc, ins, out)
    r = run_bass_kernel_spmd(nc, [{f"in_{k}": a for k, a in arrays.items()}], core_ids=[0])
    return r.results[0]["out"]
```

```python
from contextlib import ExitStack

import numpy as np

import concourse.bass as bass
from concourse import mybir

F32 = mybir.dt.float32
F32R = mybir.dt.float32r
BF16 = mybir.dt.bfloat16
U32 = mybir.dt.uint32
I32 = mybir.dt.int32
ALU = mybir.AluOpType
ACT = mybir.ActivationFunctionType
AX = mybir.AxisListType

P = 128
SEQS, LEN, D = 8, 512, 256
TOKENS = SEQS * LEN
STATE, TAPS = 16, 4
HALVES = D // P
CHPG = P // STATE
GROUPS = D // CHPG
QUADS = GROUPS // 4
SLOTS = GROUPS // 2
TT = LEN // P
EPS = 1e-5
E, TOPK, INNER = 8, 4, 512
ALPHA, LIMIT = 1.702, 7.0
TILE = 512
SUBS = TILE // P
ROW = 272
COL_TOKEN, COL_WEIGHT = D, D + 1
QUEUE = TOKENS + TILE
CH = INNER // P
KD = D // P
W_GU, W_D, W_B = KD * 2 * INNER, CH * D, 2 * CH + D
W_ALL = W_GU + W_D + W_B


class Seq:

    def __init__(self, half, off):
        self.off, self.half = off, half
        self.n = 2 * half + off
        self.p = off % 2
        self.use = half + off // 2

    def at(self, d):
        return Seq(self.half, self.off + d)


class Round:
    FIRST, LAST = -1, SEQS + 1
    LOOP = range(3, SEQS - 1)

    def __init__(self, seq, like):
        self.s, self.like = seq, like
        self.a = like + 1 < SEQS
        self.b = 0 <= like < SEQS
        self.c = 0 <= like - 1 < SEQS
        self.d = 0 <= like - 2 < SEQS
        self.next_b = 0 <= like + 1 < SEQS
        self.e = 0 <= like - 3 < SEQS - 1
        self.last = like == Round.LAST

    def blocks(self):
        d, a, c = self.d, self.a, self.c
        return (["tr0", "tr1", "rt"] * d + ["in0", "in1", "cv0"] * a + ["cnt"] * d + ["cv1"] * a + ["o0", "o1"] * c
                + ["dt0", "dt1", "bb", "cc", "in2", "in3"] * a)

    def block(self, name):
        before = sum(len(Round(Seq(0, i), i).blocks()) for i in range(Round.FIRST, self.like))
        k = before + self.blocks().index(name)
        per = len(self.blocks()) // 2
        return k % 2, k // 2 + 1 + (0 if isinstance(self.s.half, int) else per * (self.s.n - self.like))


def rounds(eng):
    lo, hi = Round.LOOP.start, Round.LOOP.stop
    for i in range(Round.FIRST, lo):
        yield Round(Seq(0, i), i)
    with eng.Fori(lo // 2, hi // 2) as half:
        for off in range(2):
            yield Round(Seq(half, lo % 2 + off), lo + off)
    for i in range(hi, Round.LAST + 1):
        yield Round(Seq(0, i), i)


def constants():
    p = np.arange(P)
    col = np.arange(P)
    c = {}
    c["pick"] = (p[:, None, None] % 64 == CHPG * np.arange(8)[None, :, None] + col[None, None, :] // STATE)
    c["gather"] = np.arange(32)[None, None, :] == CHPG * np.arange(4)[None, :, None] + p[:, None, None] // STATE
    c["ident"] = p[:, None] == col[None, :]
    c["before"] = p[:, None] < col[None, :]
    c["ones"] = np.ones((P, P))
    e = np.arange(E)
    c["lower"] = np.broadcast_to(e[None, :] < e[:, None], (P, E, E))
    c["upper"] = np.broadcast_to(e[None, :] > e[:, None], (P, E, E))
    c["slot"] = np.broadcast_to(np.arange(TOPK)[:, None], (P, TOPK, E))
    c["queue"] = np.broadcast_to(e * QUEUE, (P, E))
    c["token"] = p[:, None] + P * np.arange(TT)[None, :]
    c["spill"] = TOKENS + SUBS * p[:, None] + np.arange(SUBS)[None, :]
    c["tile"] = np.broadcast_to(np.arange(PLANNED)[:, None], (P, PLANNED, E))
    return {k: np.ascontiguousarray(np.broadcast_to(v, v.shape), dtype=np.float32).reshape(P, -1) for k, v in c.items()}


TILES = TOKENS * TOPK // TILE + E
PLANNED = TILES + 2
CONSTANTS = constants()


class Steps:

    def __init__(self, eng, sem, use, per):
        self.eng, self.sem, self.base, self.per, self.k = eng, sem, use * per, per, 0

    def then(self, ins):
        self.k += 1
        ins.then_inc(self.sem, 1)
        self.eng.wait_ge(self.sem, self.base + self.k)

    def step(self, ins):
        self.k += 1
        k = self.k
        ins.then_inc(self.sem, 1)
        yield
        self.eng.wait_ge(self.sem, self.base + k)


def weave(*chains):
    chains = list(chains)
    while chains:
        for c in list(chains):
            if next(c, "end") == "end":
                chains.remove(c)


NW = 2 * D + D + D + 2 * STATE
SMALL = (("wr", KD, E), ("gather", 4, 32), ("ident", P), ("lower", E, E), ("upper", E, E), ("slot", TOPK, E),
         ("queue", E), ("spill", SUBS), ("token", TT), ("rate", GROUPS), ("b_in", 4), ("b_conv", HALVES),
         ("b_dt", HALVES), ("skip", HALVES), ("b_bc", 2), ("taps", HALVES, TAPS), ("ln_g", D), ("ln_b", D),
         ("b_router", E))


def program(nc, ins, out):
    with ExitStack() as ctx:
        build(nc, ctx, ins, out)


def build(nc, ctx, ins, out):
    def sem(name):
        return ctx.enter_context(nc.semaphore(name))

    def sb(name, *shape, dt=F32, at=ctx):
        return at.enter_context(nc.sbuf_tensor(name, [P, *shape], dt))

    def part(tensor, at, *shape):
        n = int(np.prod(shape))
        letters = "abc"[:len(shape)]
        text = f"p ({' '.join(letters)}) -> p {' '.join(letters)}"
        return tensor[:, at:at + n].rearrange(text, **dict(zip(letters, shape)))

    def ps(name, cols, at=ctx):
        return at.enter_context(nc.psum_tensor(name, [P, cols], F32))

    queues = nc.dram_tensor("queues", [E * QUEUE + TILE, ROW], F32).ap()
    total = nc.dram_tensor("total", [TOKENS + TILE, D], F32).ap()
    GU = KD * 2 * INNER
    NWE = GU + CH * D
    total_rows = total[0:TOKENS, :].rearrange("(s t p) d -> s p t d", t=TT, p=P)
    out_rows = out.rearrange("s (t p) d -> s p t d", p=P)

    base = sb("base", E)
    small = sb("small", sum(int(np.prod(shape)) for _, *shape in SMALL))
    at, small_parts = 0, {}
    for name, *shape in SMALL:
        small_parts[name] = part(small, at, *shape)
        at += int(np.prod(shape))
    (wr, gather, ident, lower, upper, slot, c_queue, c_spill, token, rate, b_in, b_conv, b_dt, skip, b_bc, tap, ln_g,
     ln_b, b_router) = small_parts.values()
    scrap = sb("scrap", 3)
    neg_half = sb("neg_half", TT)
    expert_i = sb("expert_i", PLANNED, dt=I32)
    row_i = sb("row_i", PLANNED, dt=I32)
    base_i = sb("base_i", E, dt=I32)
    pairs_i = sb("pairs_i", 1, dt=I32)
    first_raw = sb("first_raw", W_ALL)
    first_wh = sb("first_wh", NWE, dt=F32R)
    first_wl = sb("first_wl", NWE, dt=F32R)
    first_rows = sb("first_rows", SUBS, ROW)


    one = ctx.enter_context(ExitStack())
    IN, DT_, OUT, BC = 0, 2 * D, 3 * D, 4 * D
    w_hi = sb("w_hi", KD, NW, dt=F32R, at=one)
    w_lo = sb("w_lo", KD, NW, dt=F32R, at=one)
    bc_hi = sb("bc_hi", KD, 2, P, dt=F32R, at=one)
    bc_lo = sb("bc_lo", KD, 2, P, dt=F32R, at=one)
    pick = sb("pick", 8, P, dt=F32R, at=one)
    taps = sb("taps", HALVES * TAPS, P, at=one)
    bo_hi = sb("bo_hi", D, dt=F32R, at=one)
    bo_lo = sb("bo_lo", D, dt=F32R, at=one)
    ones_r = sb("ones_r", P, dt=F32R, at=one)
    before = sb("before", P, dt=BF16, at=one)
    ones = sb("ones", P, dt=BF16, at=one)

    A = KD * LEN
    xt = part(first_raw, 0, KD, LEN)
    xt_hi = part(first_wh, 0, KD, LEN)
    xt_lo = part(first_wh, A, KD, LEN)
    x = sb("x", TT, D, at=one)
    xpad = part(first_raw, 2 * A, HALVES, TAPS - 1 + LEN)
    xc = [sb(f"xc{i}", HALVES, LEN, at=one) for i in range(2)]
    sg = [sb(f"sg{i}", HALVES, LEN, at=one) for i in range(2)]
    xc_hi = part(first_wh, 2 * A, KD, LEN)
    xc_lo = part(first_wl, 0, KD, LEN)
    relu = part(first_raw, A, HALVES, LEN)
    expo = sb("expo", HALVES, LEN, at=one)
    rest = sb("rest", HALVES, LEN, at=one)
    dt_st = [part(first_wl, A, 2 * HALVES, LEN), sb("dt_st1", 2 * HALVES, LEN, dt=F32R, at=one)]
    u_st = [sb(f"u_st{i}", 2 * HALVES, LEN, dt=F32R, at=one) for i in range(2)]
    b_rep = [sb(f"b_rep{i}", LEN, at=one) for i in range(2)]
    c_rep = [sb(f"c_rep{i}", LEN, at=one) for i in range(2)]
    decay = [sb(f"decay{i}", 2, LEN, at=one) for i in range(2)]
    state = [sb(f"state{i}", 2, LEN, at=one) for i in range(4)]
    read = [sb(f"read{i}", 4, LEN, at=one) for i in range(2)]
    y = sb("y", HALVES, LEN, at=one)
    y_hi = sb("y_hi", HALVES, LEN, dt=F32R, at=one)
    y_lo = sb("y_lo", HALVES, LEN, dt=F32R, at=one)
    z = sb("z", TT, D, at=one)
    stats = sb("stats", 2, TT, 6, at=one)
    mv = sb("mv", 2, TT, 2, at=one)
    neg_mean = sb("neg_mean", 2, TT, at=one)
    rstd = sb("rstd", 2, TT, at=one)
    rows = [sb("rows0", TT, ROW, at=one), first_rows]
    x1t = sb("x1t", KD, LEN, at=one)
    logp = x1t
    lg = sb("lg", TT, E, at=one)
    cmp = sb("cmp", 2, TT, E, E, at=one)
    rank = sb("rank", TT, E, at=one)
    chosen = sb("chosen", TT + 1, E, dt=BF16, at=one)
    top = sb("top", TT, at=one)
    ex = sb("ex", TT, E, at=one)
    den = sb("den", 2, TT, at=one)
    place = sb("place", TT, E, at=one)
    spot = sb("spot", TT, TOPK, E, at=one)
    spot_sum = sb("spot_sum", TT, TOPK, at=one)
    index = [sb(f"index{i}", TT * TOPK, dt=U32, at=one) for i in range(2)]

    pone = ctx.enter_context(ExitStack())
    p_bank = [ps(f"p_bank{i}", 512, at=pone) for i in range(2)]
    p_dt = [ps(f"p_dt{i}", LEN, at=pone) for i in range(2)]
    p_u = ps("p_u", 2 * LEN, at=pone)
    p_y = [ps(f"p_y{i}", LEN, at=pone) for i in range(2)]

    s_const = sem("s_const")
    s_set_dve, s_set_act = sem("s_set_dve"), sem("s_set_act")
    s_xt, s_x = sem("s_xt"), sem("s_x")
    bank_full = [sem(f"bank_full{i}") for i in range(2)]
    bank_read = [sem(f"bank_read{i}") for i in range(2)]
    s_xt_hi, s_xt_lo, s_silu, s_xc_hi, s_xc_lo = (sem(n) for n in ("s_xt_hi", "s_xt_lo", "s_silu", "s_xc_hi", "s_xc_lo"))
    s_exp, s_log, s_rest0, s_rest, s_sum, s_dt, s_u = (sem(n) for n in ("s_exp", "s_log", "s_rest0", "s_rest", "s_sum", "s_dt", "s_u"))
    s_hi, s_lo = sem("s_hi"), sem("s_lo")
    s_pdt, s_pu, s_decay, s_bu, s_state, s_read, s_quad = (sem(n) for n in ("s_pdt", "s_pu", "s_decay", "s_bu", "s_state", "s_read", "s_quad"))
    s_skip, s_y, s_y_hi, s_y_lo = (sem(n) for n in ("s_skip", "s_y", "s_y_hi", "s_y_lo"))
    s_norm, s_rstd, s_normed1, s_scaled, s_x1 = (sem(n) for n in ("s_norm", "s_rstd", "s_normed1", "s_scaled", "s_x1"))
    s_route, s_rexp, s_chosen, s_index = (sem(n) for n in ("s_route", "s_rexp", "s_chosen", "s_index"))
    s_scrap = sem("s_scrap")
    s_left = sem("s_left")
    s_scat = [sem(f"s_scat{i}") for i in range(2)]
    s_total = [sem(f"s_total{i}") for i in range(2)]
    s_stats, s_residual = sem("s_stats"), sem("s_residual")
    NORM_STEPS, ROUTE_STEPS = 2, 13

    raw = read[0][:, :, :].rearrange("p a b -> p (a b)")
    raw_w0, raw_w1 = raw[:, 0:NW], read[1][:, :, :].rearrange("p a b -> p (a b)")[:, 0:NW]
    raw_pick = decay[0][:, :, :].rearrange("p a b -> p (a b)")

    c_before, c_ones, b_out = state[0][:, 0, 0:P], state[0][:, 0, P:2 * P], state[0][0:1, 0, 2 * P:2 * P + D]

    loads = [(raw_w0, ins["weights"][0]), (small[:, :], ins["small"]), (raw_w1, ins["weights"][1]),
             (state[0][:, 0, :], ins["set_up"]), (raw_pick, ins["pick"])]
    SETUP = 16 * len(loads)

    def after(eng, s, n):
        if not isinstance(n, int) or n > 0:
            eng.wait_ge(s, n)

    def pair_of(t):
        quad = t // 2
        return quad, quad // 4, quad % 4, (2 * (t % 2), 2 * (t % 2) + 1)

    def flat(ap):
        return ap.rearrange("p a b -> p (a b)")

    def full(eng, r, name):
        bank, n = r.block(name)
        eng.wait_ge(bank_full[bank], n)
        return p_bank[bank], bank_read[bank]

    c_tile, past = part(flat(expo[:, :, :]), 0, PLANNED, E), part(flat(expo[:, :, :]), PLANNED * E, 2, PLANNED, E)
    t_expert, t_start, t_row, t_valid = (rest[:, 0, PLANNED * i:PLANNED * (i + 1)] for i in range(4))
    one_row, used, tiles_e, upto, first = (rest[:, 1, E * i:E * (i + 1)] for i in range(5))
    pairs_f = rest[:, 1, 5 * E:5 * E + 1]
    used_i = sb("used_i", E, dt=I32, at=one)
    pad = part(read[0][:, :, :].rearrange("p a b -> p (a b)"), 0, SUBS, ROW)
    raw_w, wh, wl, xq = [first_raw], [first_wh], [first_wl], [first_rows]
    s_rows = [sem(f"s_rows{i}") for i in range(2)]
    s_tr, s_tok, s_share = sem("s_tr"), sem("s_tok"), sem("s_share")
    s_ends = sem("s_ends")
    s_tload, s_plan, s_tables, s_pad = sem("s_tload"), sem("s_plan"), sem("s_tables"), sem("s_pad")
    s_w = [sem(f"s_w{i}") for i in range(2)]
    s_wh, s_wl, s_bias = sem("s_wh"), sem("s_wl"), sem("s_bias")
    s_gu, s_down = sem("s_gu"), sem("s_down")

    def make_padding(dve):
        dve.memset(pad[:, :, :], 0.0).then_inc(s_ends, 1)
        dve.wait_ge(s_ends, 1)
        dve.tensor_copy(pad[:, :, COL_TOKEN].bitcast(I32), c_spill[:, :]).then_inc(s_ends, 1)

    def plan(dve):
        dve.wait_ge(s_tload, 16)
        steps = Steps(dve, s_plan, 0, 15)
        dve.memset(one_row[:, :], 1.0)
        steps.then(dve.tensor_tensor(used[:, :], base[:, :], c_queue[:, :], ALU.subtract))
        steps.then(dve.tensor_scalar(used_i[:, :], used[:, :], float(TILE - 1), None, ALU.add))
        steps.then(dve.tensor_scalar(used_i[:, :], used_i[:, :], TILE.bit_length() - 1, None, ALU.arith_shift_right))
        steps.then(dve.tensor_copy(tiles_e[:, :], used_i[:, :]))
        steps.then(dve.tensor_tensor_scan(upto[:, :], one_row[:, :], tiles_e[:, :], 0.0, ALU.mult, ALU.add))
        steps.then(dve.tensor_tensor(first[:, :], upto[:, :], tiles_e[:, :], ALU.subtract))
        dve.tensor_scalar(t_valid[:, :], c_tile[:, :, 0], upto[:, E - 1:E], None, ALU.is_lt)
        dve.tensor_scalar(pairs_f[:, :], upto[:, E - 1:E], -1.0, None, ALU.add)
        for i, edge in enumerate((upto, first)):
            last = dve.tensor_tensor(past[:, i, :, :], edge[:, :].unsqueeze(1).broadcast_to([P, PLANNED, E]),
                                     c_tile[:, :, :], ALU.is_le)
        steps.then(last)
        dve.tensor_copy(pairs_i[:, :], pairs_f[:, :])
        dve.tensor_reduce(t_expert[:, :], past[:, 0, :, :], AX.X, ALU.add)
        steps.then(dve.tensor_tensor(past[:, 1, :, :], past[:, 1, :, :],
                                     first[:, :].unsqueeze(1).broadcast_to([P, PLANNED, E]), ALU.mult))
        dve.tensor_scalar(pairs_i[:, :], pairs_i[:, :], 1, None, ALU.arith_shift_right)
        dve.tensor_scalar(t_expert[:, :], t_expert[:, :], float(E - 1), None, ALU.min)
        steps.then(dve.tensor_reduce(t_start[:, :], past[:, 1, :, :], AX.X, ALU.max))
        dve.tensor_copy(expert_i[:, :], t_expert[:, :])
        dve.tensor_scalar(t_expert[:, :], t_expert[:, :], float(QUEUE), float(-E * QUEUE), ALU.mult, ALU.add)
        steps.then(dve.tensor_tensor(t_row[:, :], c_tile[:, :, 0], t_start[:, :], ALU.subtract))
        steps.then(dve.tensor_scalar(t_row[:, :], t_row[:, :], float(TILE), None, ALU.mult))
        steps.then(dve.tensor_tensor(t_row[:, :], t_row[:, :], t_expert[:, :], ALU.add))
        steps.then(dve.tensor_tensor(t_row[:, :], t_row[:, :], t_valid[:, :], ALU.mult))
        steps.then(dve.tensor_scalar(t_row[:, :], t_row[:, :], float(E * QUEUE), None, ALU.add))
        steps.then(dve.tensor_copy(row_i[:, :], t_row[:, :]))
        assert steps.k == steps.per, steps.k
        dve.memset(scrap[:, 0:1], 0.0).then_inc(s_tables, 1)

    def copy_weights(act, t, part):
        if part == 0:
            act.wait_ge(s_w[t.p], 16 * (t.use + 1))
            after(act, s_gu, CH * (t.n - 1))
        if part == 2:
            after(act, s_down, CH * (t.n - 1))
        at = slice(part * GU // 2, (part + 1) * GU // 2) if part < 2 else slice(GU, NWE)
        act.activation(wh[t.p][:, at], raw_w[t.p][:, at], ACT.Copy).then_inc(s_wh, 1)


    def rest_of_weights(pool, t, part):
        pool.wait_ge(s_wh, 3 * t.n + 2 + part)
        at = slice(0, GU) if part == 0 else slice(GU, NWE)
        pool.tensor_tensor(wl[t.p][:, at], raw_w[t.p][:, at], wh[t.p][:, at].bitcast(F32), ALU.subtract)\
            .then_inc(s_wl, 1)


    def load_weights(sp, t):
        expert = sp.value_load(expert_i[0:1, bass.ds(t.n, 1)], min_val=0, max_val=E - 1)
        after(sp, s_wl, 2 * (t.n - 1))
        after(sp, s_bias, t.n - 1)
        sp.dma_start(raw_w[t.p][:, :], ins["w_experts"][bass.ds(expert, 1), :, :].rearrange("e p c -> (e p) c"))\
          .then_inc(s_w[t.p], 16)


    def load_rows(sp, t):
        row = sp.value_load(row_i[0:1, bass.ds(t.n, 1)], min_val=0, max_val=E * QUEUE)
        after(sp, s_tok, t.n - 1)
        after(sp, s_share, t.n - 1)
        after(sp, s_tr, KD * (t.n - 1))
        sp.dma_start(xq[t.p][:, :, :], queues[bass.ds(row, TILE), :].rearrange("(p a) c -> p a c", a=SUBS))\
          .then_inc(s_rows[t.p], 16)

    def write_spare_rows(sp):
        sp.dma_start(queues[E * QUEUE:, :].rearrange("(p a) c -> p a c", a=SUBS), pad[:, :, :]).then_inc(s_pad, 16)
        sp.dma_start(total[TOKENS:, :].rearrange("(p a) d -> p a d", a=SUBS), pad[:, :, 0:D]).then_inc(s_pad, 16)

    def write_ends(sp, some):
        for e in some:
            row = sp.value_load(base_i[0:1, e:e + 1], min_val=e * QUEUE, max_val=e * QUEUE + TOKENS)
            sp.dma_start(queues[bass.ds(row, TILE), :].rearrange("(p a) c -> p a c", a=SUBS), pad[:, :, :]).then_inc(s_pad, 16)

    def pe_stage1(pe):
        pe.wait_ge(s_const, SETUP)
        pe.wait_ge(s_set_dve, 2)

        def block(r, name):
            bank, n = r.block(name)
            after(pe, bank_read[bank], n - 1)
            return p_bank[bank], bank_full[bank]

        def product(out, hi, lo, rhs_hi, rhs_lo, stop=True):
            for k in range(KD):
                for n, (a, b) in enumerate(((hi, rhs_hi), (hi, rhs_lo), (lo, rhs_hi))):
                    mm = pe.matmul(out, a(k), b(k), start=(k == 0 and n == 0),
                                   stop=(k == KD - 1 and n == 2 and stop))
            return mm

        def weight(at, n, part):
            return lambda k: part[:, k, at:at + n]

        def project(r, m):
            bank, done = block(r, f"in{m}")
            if m == 0:
                pe.wait_ge(s_xt_hi, r.s.at(1).n + 1)
                pe.wait_ge(s_xt_lo, r.s.at(1).n + 1)
            at = IN + m * P
            product(bank[:, :], weight(at, P, w_hi), weight(at, P, w_lo),
                    lambda k: xt_hi[:, k, :], lambda k: xt_lo[:, k, :]).then_inc(done, 1)

        def convolve(r, h, some):
            if 0 in some:
                bank, _ = block(r, f"cv{h}")
                src, n = r.block(f"in{h}")
                pe.wait_ge(bank_read[src], n)
            b, _ = r.block(f"cv{h}")
            for j in some:
                mm = pe.matmul(p_bank[b][:, :], taps[:, TAPS * h + j, :], xpad[:, h, j:j + LEN],
                               start=(j == 0), stop=(j == TAPS - 1))
            if TAPS - 1 in some:
                mm.then_inc(bank_full[b], 1)

        def from_xc(r, name, hi, lo):
            bank, done = block(r, name)
            if name == "dt0":
                pe.wait_ge(s_xc_hi, r.s.at(1).n + 1)
                pe.wait_ge(s_xc_lo, r.s.at(1).n + 1)
            product(bank[:, :], hi, lo, lambda k: xc_hi[:, k, :], lambda k: xc_lo[:, k, :]).then_inc(done, 1)

        def replicate(s, t):
            quad, half, j, tiles = pair_of(t)
            if t == 0:
                pe.wait_ge(s_hi, 2 * s.n + 2)
                pe.wait_ge(s_lo, s.n + 1)
            q = 2 * half + t % 2
            for i, c in enumerate(tiles):
                which = j + 4 * (c % 2)
                if i == 0:
                    after(pe, s_bu, SLOTS * s.n + t)
                mm = pe.matmul(p_u[:, i * LEN:(i + 1) * LEN], pick[:, which, :], u_st[s.p][:, q, :],
                               start=True, stop=True)
            mm.then_inc(s_pu, 1)
            for i, c in enumerate(tiles):
                which = j + 4 * (c % 2)
                after(pe, s_decay, GROUPS * s.n + 2 * t + i - 1)
                pe.matmul(p_dt[i][:, :], pick[:, which, :], dt_st[s.p][:, q, :], start=True, stop=True).then_inc(s_pdt, 1)

        def sum_states(s, quad):
            half, j = quad // 4, quad % 4
            pe.wait_ge(s_read, SLOTS * s.n + 2 * quad + 2)
            if j == 0:
                after(pe, s_skip, 2 * s.n + half - 1)
            for c in range(4):
                mm = pe.matmul(p_y[half][32 * c:32 * c + 32, :], gather[:, j, :], read[quad % 2][:, c, :],
                               start=(j == 0), stop=(j == 3))
            mm.then_inc(s_quad, 1)

        def project_out(r, b):
            bank, done = block(r, f"o{b}")
            s = r.s.at(-1)
            if b == 0:
                pe.wait_ge(s_y_hi, s.n + 1)
                pe.wait_ge(s_y_lo, s.n + 1)
            for i in range(2):
                to = bank[:, i * D:(i + 1) * D]
                at = (2 * b + i) * P
                product(to, lambda k: y_hi[:, k, at:at + P], lambda k: y_lo[:, k, at:at + P],
                        lambda k: w_hi[:, k, OUT:OUT + D], lambda k: w_lo[:, k, OUT:OUT + D], stop=False)
                pe.matmul(to, ones_r[0:1, :], bo_hi[0:1, :], start=False, stop=False)
                mm = pe.matmul(to, ones_r[0:1, :], bo_lo[0:1, :], start=False, stop=True)
            mm.then_inc(done, 1)

        def transpose_rows(r, k):
            bank, done = block(r, f"tr{k}")
            s = r.s.at(-2)
            pe.wait_ge(s_x1, s.n + 1)
            for t in range(TT):
                mm = pe.transpose(bank[:, t * P:(t + 1) * P], rows[s.p][:, t, k * P:(k + 1) * P], ident[:, :])
            mm.then_inc(done, 1)

        def route(r):
            bank, done = block(r, "rt")
            for k in range(KD):
                src, n = r.block(f"tr{k}")
                pe.wait_ge(bank_read[src], n)
            for t in range(TT):
                for k in range(KD):
                    mm = pe.matmul(bank[:, t * E:(t + 1) * E], x1t[:, k, t * P:(t + 1) * P], wr[:, k, :],
                                   start=(k == 0), stop=(k == KD - 1))
            mm.then_inc(done, 1)

        def count(r):
            bank, done = block(r, "cnt")
            pe.wait_ge(s_chosen, r.s.at(-2).n + 1)
            pe.matmul(bank[:, 0:(TT + 1) * E], before[:, :], flat(chosen[:, :, :]), start=True, stop=False,
                      skip_group_check=True)
            for t in range(TT):
                n = TT - t
                mm = pe.matmul(bank[:, (t + 1) * E:(TT + 1) * E], ones[:, :],
                               chosen[:, t:t + 1, :].broadcast_to([P, n, E]), start=False, stop=(t == TT - 1),
                               skip_group_check=True)
            mm.then_inc(done, 1)

        for r in rounds(pe):
            for t in range(SLOTS):
                if r.b and t < SLOTS - 1:
                    replicate(r.s, t + 1)
                if r.next_b and t == SLOTS - 1:
                    replicate(r.s.at(1), 0)
                if t in (0, 2) and r.c:
                    sum_states(r.s.at(-1), QUADS - 2 + t // 2)
                if t >= 4 and t % 2 == 0 and r.b:
                    sum_states(r.s, t // 2 - 2)
                if r.d and t == 0:
                    transpose_rows(r, 0)
                    transpose_rows(r, 1)
                if r.d and t == 1:
                    route(r)
                if r.a and t == 2:
                    project(r, 0)
                    project(r, 1)
                if r.a and t == 3:
                    convolve(r, 0, range(TAPS))
                if r.d and t == 3:
                    count(r)
                if r.a and t in (4, 5):
                    half = TAPS // 2 * (t - 4)
                    convolve(r, 1, range(half, half + TAPS // 2))
                if r.c and t in (6, 7):
                    project_out(r, t - 6)
                if r.a and t == 8:
                    for i in range(HALVES):
                        at = DT_ + i * P
                        from_xc(r, f"dt{i}", weight(at, P, w_hi), weight(at, P, w_lo))
                if r.like == Round.FIRST and t == 9:
                    pe.wait_ge(s_set_dve, SET_DVE)
                if r.a and t == 9:
                    for i in range(2):
                        from_xc(r, ("bb", "cc")[i], lambda k: bc_hi[:, k, i, :], lambda k: bc_lo[:, k, i, :])
                if r.a and t in (10, 11):
                    project(r, t - 8)

    def act_stage1(act):
        act.wait_ge(s_const, SETUP)
        act.activation(rate[:, :], rate[:, :], ACT.Exp).then_inc(s_set_act, 1)

        def split_x(s):
            act.wait_ge(s_xt, 16 * (s.n + 1))
            act.activation(flat(xt_hi[:, :, :]), flat(xt[:, :, :]), ACT.Copy).then_inc(s_xt_hi, 1)

        def store_in(r, m):
            s = r.s.at(1)
            bank, done = full(act, r, f"in{m}")
            if m == 2:
                after(act, s_y, s.n - 1)
            to = xpad[:, m, TAPS - 1:TAPS - 1 + LEN] if m < 2 else sg[s.p][:, m - 2, :]
            act.activation(to, bank[:, :], ACT.Identity, bias=b_in[:, m:m + 1]).then_inc(done, 1)

        def store_conv(r, h):
            s = r.s.at(1)
            bank, done = full(act, r, f"cv{h}")
            after(act, s_skip, 2 * (s.n - 1))
            act.activation(xc[s.p][:, h, :], bank[:, :], ACT.Identity, bias=b_conv[:, h:h + 1]).then_inc(done, 1)

        def silu(r):
            s = r.s.at(1)
            for name in ("cv0", "cv1"):
                bank, n = r.block(name)
                act.wait_ge(bank_read[bank], n)
            act.activation(flat(xc[s.p][:, :, :]), flat(xc[s.p][:, :, :]), ACT.Silu).then_inc(s_silu, 1)

        def silu_gate(r):
            s = r.s.at(1)
            for name in ("in2", "in3"):
                bank, n = r.block(name)
                act.wait_ge(bank_read[bank], n)
            act.activation(flat(sg[s.p][:, :, :]), flat(sg[s.p][:, :, :]), ACT.Silu).then_inc(s_silu, 1)

        def split_xc(r):
            s = r.s.at(1)
            act.wait_ge(s_silu, 2 * s.n + 1)
            act.activation(flat(xc_hi[:, :, :]), flat(xc[s.p][:, :, :]), ACT.Copy).then_inc(s_xc_hi, 1)

        def store_dt(r, h):
            bank, done = full(act, r, f"dt{h}")
            if h == 0:
                after(act, s_lo, r.s.at(1).n)
            act.activation(relu[:, h, :], bank[:, :], ACT.Relu, bias=b_dt[:, h:h + 1])
            act.activation(expo[:, h, :], bank[:, :], ACT.Abs, bias=b_dt[:, h:h + 1]).then_inc(done, 1)

        def softplus(r):
            s = r.s.at(1)
            bank, n = r.block("dt1")
            act.wait_ge(bank_read[bank], n)
            act.activation(flat(expo[:, :, :]), flat(expo[:, :, :]), ACT.Exp, scale=-1.0).then_inc(s_exp, 1)
            act.wait_ge(s_exp, s.n + 1)
            if r.d:
                full(act, r, "rt")
            act.activation(flat(logp[:, :, :]), flat(expo[:, :, :]), ACT.Ln, bias=1.0).then_inc(s_log, 1)

        def store_bc(r, i):
            s = r.s.at(1)
            bank, done = full(act, r, ("bb", "cc")[i])
            after(act, s_read, SLOTS * (s.n - 1))
            to = (b_rep, c_rep)[i][s.p]
            act.activation(to[:, :], bank[:, :], ACT.Identity, bias=b_bc[:, i:i + 1]).then_inc(done, 1)

        def split_scan_inputs(r):
            s = r.s.at(1)
            act.wait_ge(s_dt, s.n + 1)
            act.wait_ge(s_u, s.n + 1)
            after(act, s_pu, SLOTS * (s.n - 1))
            for st, src in ((dt_st, expo), (u_st, relu)):
                act.activation(st[s.p][0:64, 0::2, :], src[0:64, :, :], ACT.Copy)
                act.activation(st[s.p][64:128, 1::2, :], src[64:128, :, :], ACT.Copy).then_inc(s_hi, 1)

        def decays(s, t):
            quad, half, j, tiles = pair_of(t)
            after(act, s_state, SLOTS * s.n + t - 1)
            for i, c in enumerate(tiles):
                act.wait_ge(s_pdt, GROUPS * s.n + 2 * t + i + 1)
                g = 16 * half + j + 4 * c
                act.activation(decay[t % 2][:, i, 1:LEN], p_dt[i][:, 1:LEN], ACT.Exp, scale=rate[:, g:g + 1])\
                   .then_inc(s_decay, 1)

        def split_y(r):
            s = r.s.at(-1)
            act.wait_ge(s_y, s.n + 1)
            after(act, s_x1, s.n)
            act.activation(flat(y_hi[:, :, :]), flat(y[:, :, :]), ACT.Copy).then_inc(s_y_hi, 1)

        def load_x(r):
            s = r.s
            after(act, s_residual, s.n - 1)
            act.dma_start(x[:, :, :], ins["x"][bass.ds(s.n, 1), :, :].rearrange("s (t p) d -> (s p) t d", p=P))\
               .then_inc(s_x, 16)

        def start_total(r):
            s = r.s.at(-1)
            act.wait_ge(s_x1, s.n + 1)
            act.dma_start(total_rows[bass.ds(s.n, 1), :, :, :].rearrange("s p t d -> (s p) t d"),
                          rows[s.p][:, :, 0:D]).then_inc(s_total[s.p], 16)

        def apply_norm(s, which, to, done):
            act.wait_ge(s_rstd, 4 * s.n + 2 * which + 2)
            for t in range(TT):
                last = act.activation(to[:, t, 0:D], z[:, t, :], ACT.Identity, bias=neg_mean[:, which, t:t + 1],
                                      scale=rstd[:, which, t:t + 1])
            last.then_inc(done, 1)

        def second_norm(r):
            s = r.s.at(-1)
            after(act, s_left, s.n)
            apply_norm(s, 1, rows[s.p], s_x1)

        def store_x1t(r, k):
            bank, done = full(act, r, f"tr{k}")
            act.wait_ge(s_sum, SEQS if not r.a else r.s.n + 1)
            act.activation(x1t[:, k, :], bank[:, :], ACT.Copy).then_inc(done, 1)

        def router_exp(r):
            s = r.s.at(-2)
            act.wait_ge(s_rexp, 2 * s.n + 1)
            act.activation(flat(ex[:, :, :]), flat(ex[:, :, :]), ACT.Exp).then_inc(s_rexp, 1)

        for r in rounds(act):
            for t in range(SLOTS):
                if r.a and t == 0:
                    split_x(r.s.at(1))
                if r.d and t == 3:
                    router_exp(r)
                if r.c and t == 4:
                    split_y(r)
                if r.a and t == 6:
                    store_conv(r, 1)
                    silu(r)
                    split_xc(r)
                if r.a and t == 9:
                    softplus(r)
                if r.a and t in (11, 12):
                    store_in(r, t - 9)
                if r.a and t == 12:
                    split_scan_inputs(r)
                if r.a and t == 14:
                    silu_gate(r)
                if r.b and t < SLOTS - 1:
                    decays(r.s, t + 1)
                if r.like == Round.FIRST and t == SLOTS - 1:
                    act.wait_ge(s_set_dve, SET_DVE)
                if r.next_b and t == SLOTS - 1:
                    decays(r.s.at(1), 0)
                if r.d and t == 0:
                    store_x1t(r, 0)
                    store_x1t(r, 1)
                if r.a and t == 2:
                    store_in(r, 0)
                    store_in(r, 1)
                if r.a and t == 3:
                    store_conv(r, 0)
                if r.a and t == 8:
                    store_dt(r, 0)
                    store_dt(r, 1)
                if r.a and t == 9:
                    store_bc(r, 0)
                    store_bc(r, 1)
                if r.c and t == 9:
                    apply_norm(r.s.at(-1), 0, z, s_normed1)
                if r.b and t == 14:
                    load_x(r)
                if r.c and t == 14:
                    second_norm(r)
                if r.c and t == 15:
                    start_total(r)

    SET_DVE = 4

    def dve_setup(dve):
        dve.wait_ge(s_const, SETUP)
        dve.tensor_copy(w_hi[:, 0, :], raw_w0)
        dve.tensor_copy(w_hi[:, 1, :], raw_w1).then_inc(s_set_dve, 1)
        for i in range(HALVES * TAPS):
            dve.tensor_scalar(taps[:, i, :], ident[:, :], tap[:, i // TAPS, i % TAPS:i % TAPS + 1], None, ALU.mult)
        for h in range(2):
            dve.memset(xpad[:, h, 0:TAPS - 1], 0.0)
        dve.wait_ge(s_set_dve, 1)
        dve.tensor_tensor(w_lo[:, 0, :], raw_w0, w_hi[:, 0, :].bitcast(F32), ALU.subtract)
        dve.tensor_tensor(w_lo[:, 1, :], raw_w1, w_hi[:, 1, :].bitcast(F32), ALU.subtract).then_inc(s_set_dve, 1)

    def dve_setup_rest(dve):
        dve.wait_ge(s_set_dve, 2)
        dve.memset(neg_half[:, :], -0.5)
        dve.tensor_copy(base[:, :], c_queue[:, :])
        dve.tensor_copy(bo_hi[0:1, :], b_out)
        dve.tensor_copy(ones_r[:, :], c_ones)
        dve.tensor_copy(flat(pick[:, :, :]), raw_pick)
        dve.tensor_copy(before[:, :], c_before)
        dve.tensor_copy(ones[:, :], c_ones)
        dve.memset(scrap[:, 2:3], 0.0).then_inc(s_left, 1)
        dve.memset(chosen[:, :, :], 0.0)
        for k in range(KD):
            for half, to in ((w_hi, bc_hi), (w_lo, bc_lo)):
                for i in range(2):
                    src = half[:, k, BC + STATE * i:BC + STATE * (i + 1)].bitcast(F32)
                    dve.tensor_copy(to[:, k, i, :].rearrange("p (r n) -> p r n", n=STATE),
                                    src.unsqueeze(1).broadcast_to([P, CHPG, STATE]))
        for h in range(2):
            last = dve.memset(rows[h][:, :, :], 0.0)
        last.then_inc(s_set_dve, 1)
        dve.wait_ge(s_set_dve, 3)
        dve.tensor_tensor(bo_lo[0:1, :], b_out, bo_hi[0:1, :].bitcast(F32), ALU.subtract)
        for h in range(2):
            dve.memset(decay[h][:, :, 0:1], 0.0)
        dve.wait_ge(s_set_act, 1)
        dve.tensor_scalar(rate[:, :], rate[:, :], -1.0, None, ALU.mult).then_inc(s_set_dve, 1)

    def dve_stage1(dve):
        dve_setup(dve)

        def f32(ap):
            return ap.bitcast(F32)

        def split_x(s):
            dve.wait_ge(s_xt_hi, s.n + 1)
            after(dve, s_xc_hi, s.n)
            dve.tensor_tensor(flat(xt_lo[:, :, :]), flat(xt[:, :, :]), f32(flat(xt_hi[:, :, :])), ALU.subtract)\
               .then_inc(s_xt_lo, 1)

        def split_xc(r):
            s = r.s.at(1)
            dve.wait_ge(s_xc_hi, s.n + 1)
            dve.tensor_tensor(flat(xc_lo[:, :, :]), flat(xc[s.p][:, :, :]), f32(flat(xc_hi[:, :, :])), ALU.subtract)\
               .then_inc(s_xc_lo, 1)

        def softplus_rest(r):
            s = r.s.at(1)
            dve.wait_ge(s_exp, s.n + 1)
            dve.tensor_scalar(flat(rest[:, :, :]), flat(expo[:, :, :]), 1.0, -1.0, ALU.add, ALU.add).then_inc(s_rest0, 1)
            dve.wait_ge(s_log, s.n + 1)
            dve.tensor_tensor(flat(relu[:, :, :]), flat(relu[:, :, :]), flat(logp[:, :, :]), ALU.add).then_inc(s_sum, 1)
            dve.wait_ge(s_rest0, s.n + 1)
            dve.tensor_tensor(flat(rest[:, :, :]), flat(expo[:, :, :]), flat(rest[:, :, :]), ALU.subtract)\
               .then_inc(s_rest, 1)

        def scan_inputs(r):
            s = r.s.at(1)
            dve.wait_ge(s_sum, s.n + 1)
            dve.wait_ge(s_rest, s.n + 1)
            dve.tensor_tensor(flat(expo[:, :, :]), flat(relu[:, :, :]), flat(rest[:, :, :]), ALU.add).then_inc(s_dt, 1)
            dve.wait_ge(s_dt, s.n + 1)
            dve.tensor_tensor(flat(relu[:, :, :]), flat(expo[:, :, :]), flat(xc[s.p][:, :, :]), ALU.mult).then_inc(s_u, 1)

        def split_scan_inputs(r, which):
            s = r.s.at(1)
            dve.wait_ge(s_hi, 2 * s.n + which + 1)
            st, src = ((dt_st, expo), (u_st, relu))[which]
            dve.tensor_tensor(st[s.p][64:128, 0::2, :], src[0:64, :, :], f32(st[s.p][0:64, 0::2, :]), ALU.subtract)
            last = dve.tensor_tensor(st[s.p][0:64, 1::2, :], src[64:128, :, :], f32(st[s.p][64:128, 1::2, :]),
                                     ALU.subtract)
            if which == 1:
                last.then_inc(s_lo, 1)

        def weigh_inputs(r, t):
            s = r.s
            if t == 0:
                dve.wait_ge(s_hi, 2 * s.n + 2)
            dve.wait_ge(s_pu, SLOTS * s.n + t + 1)
            after(dve, s_read, SLOTS * s.n + t - 3)
            u = p_u[:, :].rearrange("p (a b) -> p a b", a=2)
            dve.tensor_tensor(state[t % 4][:, :, :], u, b_rep[s.p][:, :].unsqueeze(1).broadcast_to([P, 2, LEN]), ALU.mult).then_inc(s_bu, 1)

        def scan(s, t):
            n = SLOTS * s.n + t
            dve.wait_ge(s_bu, n + 1)
            dve.wait_ge(s_decay, 2 * n + 2)
            dve.tensor_tensor_scan(flat(state[t % 4][:, :, :]), flat(decay[t % 2][:, :, :]),
                                   flat(state[t % 4][:, :, :]), 0.0, ALU.mult, ALU.add).then_inc(s_state, 1)

        def skip_path(s, h):
            dve.wait_ge(s_quad, QUADS * s.n + 4 * h + 4)
            dve.scalar_tensor_tensor(y[:, h, :], xc[s.p][:, h, :], skip[:, h:h + 1], p_y[h][:, :], ALU.mult, ALU.add)\
               .then_inc(s_skip, 1)

        def gate(r):
            s = r.s.at(-1)
            dve.wait_ge(s_skip, 2 * s.n + 2)
            dve.tensor_tensor(flat(y[:, :, :]), flat(y[:, :, :]), flat(sg[s.p][:, :, :]), ALU.mult).then_inc(s_y, 1)

        def split_y(r):
            s = r.s.at(-1)
            dve.wait_ge(s_y_hi, s.n + 1)
            dve.tensor_tensor(flat(y_lo[:, :, :]), flat(y[:, :, :]), f32(flat(y_hi[:, :, :])), ALU.subtract)\
               .then_inc(s_y_lo, 1)

        def add_input(r, b):
            s = r.s.at(-1)
            bank, done = full(dve, r, f"o{b}")
            if b == 0:
                dve.wait_ge(s_x, 16 * (s.n + 1))
            dve.tensor_tensor(flat(z[:, 2 * b:2 * b + 2, :]), bank[:, :], flat(x[:, 2 * b:2 * b + 2, :]), ALU.add)\
               .then_inc(done, 1)

        def statistics(s, which):
            for t in range(TT):
                last = dve.bn_stats(stats[:, which, t, :], z[:, t, :])
            last.then_inc(s_stats, 1)

        def moments(s, which):
            steps = Steps(dve, s_norm, 2 * s.n + which, NORM_STEPS)
            dve.wait_ge(s_stats, 2 * s.n + which + 1)
            dve.memset(scrap[:, 0:1], 0.0)
            for t in range(TT):
                last = dve.bn_aggr(mv[:, which, t, :], stats[:, which, t, :])
            yield from steps.step(last)
            dve.tensor_scalar(mv[:, which, :, 1], mv[:, which, :, 1], EPS, None, ALU.add)
            yield from steps.step(dve.tensor_scalar(neg_mean[:, which, :], mv[:, which, :, 0], -1.0, None, ALU.mult))
            assert steps.k == steps.per, steps.k

        def first_statistics(r):
            s = r.s.at(-1)
            for b in range(2):
                bank, n = r.block(f"o{b}")
                dve.wait_ge(bank_read[bank], n)
            statistics(s, 0)

        def residual(r):
            s = r.s.at(-1)
            dve.wait_ge(s_scaled, s.n + 1)
            dve.tensor_tensor(flat(z[:, :, :]), flat(z[:, :, :]), flat(x[:, :, :]), ALU.add).then_inc(s_residual, 1)
            dve.wait_ge(s_residual, s.n + 1)
            statistics(s, 1)

        def rank_experts(r, steps):
            s = r.s.at(-2)
            bank, done = full(dve, r, "rt")
            dve.tensor_tensor(lg[:, :, :], bank[:, 0:TT * E].rearrange("p (t e) -> p t e", e=E),
                              b_router[:, :].unsqueeze(1).broadcast_to([P, TT, E]), ALU.add).then_inc(done, 1)
            b, n = r.block("rt")
            dve.wait_ge(bank_read[b], n)
            other = lg[:, :, :].unsqueeze(2).broadcast_to([P, TT, E, E])
            own = lg[:, :, :].unsqueeze(3).broadcast_to([P, TT, E, E])
            dve.tensor_tensor(cmp[:, 0, :, :, :], other, own, ALU.is_ge)
            yield from steps.step(dve.tensor_tensor(cmp[:, 1, :, :, :], other, own, ALU.is_gt))
            dve.tensor_tensor(cmp[:, 0, :, :, :], cmp[:, 0, :, :, :], lower[:, :, :].unsqueeze(1).broadcast_to([P, TT, E, E]), ALU.mult)
            yield from steps.step(dve.tensor_tensor(cmp[:, 1, :, :, :], cmp[:, 1, :, :, :], upper[:, :, :].unsqueeze(1).broadcast_to([P, TT, E, E]), ALU.mult))
            yield from steps.step(dve.tensor_tensor(cmp[:, 0, :, :, :], cmp[:, 0, :, :, :], cmp[:, 1, :, :, :], ALU.add))
            dve.tensor_reduce(top[:, :], lg[:, :, :], AX.X, ALU.max)
            yield from steps.step(dve.tensor_reduce(rank[:, :, :], cmp[:, 0, :, :, :], AX.X, ALU.add))
            dve.tensor_scalar(chosen[:, 0:TT, :], rank[:, :, :], float(TOPK), None, ALU.is_lt).then_inc(s_chosen, 1)
            dve.tensor_tensor(ex[:, :, :], lg[:, :, :], top[:, :].unsqueeze(2).broadcast_to([P, TT, E]), ALU.subtract)\
               .then_inc(s_rexp, 1)

        def weigh_experts(r, steps):
            s = r.s.at(-2)
            dve.wait_ge(s_rexp, 2 * s.n + 2)
            dve.wait_ge(s_chosen, s.n + 1)
            yield from steps.step(dve.tensor_tensor(ex[:, :, :], ex[:, :, :], chosen[:, 0:TT, :], ALU.mult))
            yield from steps.step(dve.tensor_reduce(den[:, 0, :], ex[:, :, :], AX.X, ALU.add))
            yield from steps.step(dve.reciprocal(den[:, 1, :], den[:, 0, :]))
            dve.tensor_tensor(rows[s.p][:, :, COL_WEIGHT:COL_WEIGHT + E], ex[:, :, :],
                              den[:, 1, :].unsqueeze(2).broadcast_to([P, TT, E]), ALU.mult)
            yield from steps.step(dve.tensor_copy(rows[s.p][:, :, COL_TOKEN].bitcast(I32), token[:, :]))
            yield from steps.step(dve.tensor_scalar(token[:, :], token[:, :], float(LEN), None, ALU.add))

        def take_counts(r, steps):
            bank, done = full(dve, r, "cnt")
            steps.then(dve.tensor_tensor(place[:, :, :], bank[:, 0:TT * E].rearrange("p (t e) -> p t e", e=E),
                                         base[:, :].unsqueeze(1).broadcast_to([P, TT, E]), ALU.add))
            dve.tensor_tensor(base[:, :], base[:, :], bank[:, TT * E:(TT + 1) * E], ALU.add).then_inc(done, 1)

        def places(r, steps):
            s = r.s.at(-2)
            yield from steps.step(dve.tensor_tensor(spot[:, :, :, :], rank[:, :, :].unsqueeze(2).broadcast_to([P, TT, TOPK, E]),
                                         slot[:, :, :].unsqueeze(1).broadcast_to([P, TT, TOPK, E]), ALU.is_equal))
            yield from steps.step(dve.tensor_tensor(spot[:, :, :, :], spot[:, :, :, :],
                                         place[:, :, :].unsqueeze(2).broadcast_to([P, TT, TOPK, E]), ALU.mult))
            yield from steps.step(dve.tensor_reduce(spot_sum[:, :, :], spot[:, :, :, :], AX.X, ALU.add))

        def scan_slot(r, t):
            if r.b:
                weigh_inputs(r, t)
                yield
            if t == 0 and r.c:
                scan(r.s.at(-1), SLOTS - 1)
            if t > 0 and r.b:
                scan(r.s, t - 1)

        for r in rounds(dve):
            for t in range(SLOTS):
                if r.like == Round.FIRST and t == 2:
                    dve_setup_rest(dve)
                if r.d and t == 2:
                    route_steps = Steps(dve, s_route, r.s.at(-2).n, ROUTE_STEPS)
                    weave(scan_slot(r, t), rank_experts(r, route_steps))
                elif r.c and t == 13:
                    weave(scan_slot(r, t), moments(r.s.at(-1), 1))
                else:
                    weave(scan_slot(r, t))
                if r.a and t == 1:
                    split_x(r.s.at(1))
                if r.c and t == 3:
                    skip_path(r.s.at(-1), 1)
                    gate(r)
                if r.d and t == 4:
                    take_counts(r, route_steps)
                if r.c and t == 5:
                    split_y(r)
                if r.last and t == 0:
                    make_padding(dve)
                if r.last and t == 4:
                    b, n = r.block("cnt")
                    dve.wait_ge(bank_read[b], n)
                    dve.tensor_copy(base_i[:, :], base[:, :]).then_inc(s_ends, 1)
                if r.d and t == 5:
                    weave(weigh_experts(r, route_steps), places(r, route_steps))
                    assert route_steps.k == ROUTE_STEPS
                    dve.tensor_copy(index[r.s.at(-2).p][:, :], flat(spot_sum[:, :, :])).then_inc(s_index, 1)
                if r.a and t == 7:
                    split_xc(r)
                if r.c and t in (7, 8):
                    add_input(r, t - 7)
                if r.c and t == 8:
                    first_statistics(r)
                    weave(moments(r.s.at(-1), 0))
                if r.a and t == 10:
                    softplus_rest(r)
                if r.b and t == 11:
                    skip_path(r.s, 0)
                if r.a and t == 11:
                    scan_inputs(r)
                if r.c and t == 12:
                    residual(r)
                if r.a and t == 13:
                    split_scan_inputs(r, 0)
                if r.a and t == 14:
                    split_scan_inputs(r, 1)

    def pool_stage1(pool):
        pool.wait_ge(s_set_dve, SET_DVE)

        def read_state(s, t):
            quad, _, _, tiles = pair_of(t)
            n = SLOTS * s.n + t
            pool.wait_ge(s_state, n + 1)
            after(pool, s_quad, QUADS * s.n + quad - 1)
            pool.tensor_tensor(read[quad % 2][:, tiles[0]:tiles[0] + 2, :], state[t % 4][:, :, :],
                               c_rep[s.p][:, :].unsqueeze(1).broadcast_to([P, 2, LEN]), ALU.mult).then_inc(s_read, 1)

        def power(s, which):
            pool.wait_ge(s_norm, NORM_STEPS * (2 * s.n + which + 1))
            pool.tensor_tensor(rstd[:, which, :], mv[:, which, :, 1], neg_half[:, :], ALU.pow).then_inc(s_rstd, 1)
            pool.wait_ge(s_rstd, 4 * s.n + 2 * which + 1)
            pool.tensor_tensor(neg_mean[:, which, :], neg_mean[:, which, :], rstd[:, which, :], ALU.mult)\
                .then_inc(s_rstd, 1)

        def scale(r):
            s = r.s.at(-1)
            pool.wait_ge(s_normed1, s.n + 1)
            pool.tensor_tensor(z[:, :, :], z[:, :, :], ln_g[:, :].unsqueeze(1).broadcast_to([P, TT, D]), ALU.mult)\
                .then_inc(s_scaled, 1)

        def add_offset(r):
            pool.wait_ge(s_stats, 2 * r.s.at(-1).n + 1)
            pool.tensor_tensor(x[:, :, :], x[:, :, :], ln_b[:, :].unsqueeze(1).broadcast_to([P, TT, D]), ALU.add)

        def scatter(s, some):
            if 0 in some:
                pool.wait_ge(s_index, s.n + 1)
                after(pool, s_scrap, s.n)
                pool.tensor_tensor(scrap[:, 1:2], neg_half[:, 0:1], neg_half[:, 0:1], ALU.mult).then_inc(s_scrap, 1)
            for i in some:
                pool.indirect_dma_start(queues, bass.IndirectOffsetOnAxis(ap=index[s.p][:, i:i + 1], axis=0),
                                        rows[s.p][:, i // TOPK, :], None).then_inc(s_scat[s.p], 16)

        SCATTERS_BEFORE = {7: (1,), 10: (3, 4), 13: (5, 6)}
        SCATTERS_AFTER = {6: (0,), 8: (2,), 14: (7,), 15: (8,)}

        def release_rows(r):
            s = r.s.at(-3)
            pool.wait_ge(s_scat[s.p], 16 * TT * TOPK * (s.use + 1))
            pool.wait_ge(s_total[s.p], 16 * (s.use + 1))
            pool.wait_ge(s_left, s.n + 1)
            pool.tensor_tensor(scrap[:, 2:3], neg_half[:, 0:1], neg_half[:, 0:1], ALU.mult).then_inc(s_left, 1)

        for r in rounds(pool):
            for t in range(SLOTS):
                if r.d and t in SCATTERS_BEFORE:
                    scatter(r.s.at(-2), SCATTERS_BEFORE[t])
                if t == 0 and r.c:
                    read_state(r.s.at(-1), SLOTS - 1)
                if t > 0 and r.b:
                    read_state(r.s, t - 1)
                if r.e and t < 7:
                    scatter(r.s.at(-3), range(t + 9, t + 10))
                if r.d and t in SCATTERS_AFTER:
                    scatter(r.s.at(-2), SCATTERS_AFTER[t])
                if r.e and t == 7:
                    release_rows(r)
                if r.c and t == 9:
                    power(r.s.at(-1), 0)
                    add_offset(r)
                if r.c and t == 10:
                    scale(r)
                if r.c and t == 13:
                    power(r.s.at(-1), 1)
            if r.last:
                scatter(r.s.at(-2), range(9, TT * TOPK))

    def sp_stage1(sp):

        def load_sequence(s):
            after(sp, s_xt_lo, s.n)
            sp.dma_start(xt[:, :, :], ins["x_t"][bass.ds(s.n, 1), :, :].rearrange("s (k p) l -> (s p) k l", p=P))\
              .then_inc(s_xt, 16)

        load_sequence(Seq(0, 0))
        for to, src in loads:
            sp.dma_start(to, src).then_inc(s_const, 16)
        load_sequence(Seq(0, 1))
        with sp.Fori(1, SEQS // 2) as half:
            for s in range(2):
                load_sequence(Seq(half, s))

    with nc.Block() as block:
        @block.tensor
        def _(pe):
            pe_stage1(pe)

        @block.scalar
        def _(act):
            act_stage1(act)
            for i in range(3):
                copy_weights(act, Seq(0, 0), i)

        @block.vector
        def _(dve):
            dve_stage1(dve)
            plan(dve)

        @block.gpsimd
        def _(pool):
            pool_stage1(pool)
            rest_of_weights(pool, Seq(0, 0), 0)

        @block.sync
        def _(sp):
            sp_stage1(sp)
            sp.wait_ge(s_lo, SEQS)
            sp.dma_start(c_tile.rearrange("p a b -> p (a b)"), ins["tile"]).then_inc(s_tload, 16)
            sp.wait_ge(s_ends, 2)
            write_spare_rows(sp)
            sp.wait_ge(s_ends, 3)
            write_ends(sp, range(E // 2))
            sp.wait_ge(s_tables, 1)
            load_weights(sp, Seq(0, 0))
            write_ends(sp, range(E // 2, E))
            for i in range(2):
                sp.wait_ge(s_total[i], 16 * (SEQS // 2))
                sp.wait_ge(s_scat[i], 16 * TT * TOPK * (SEQS // 2))
            sp.wait_ge(s_pad, 16 * (E + 2))
            load_rows(sp, Seq(0, 0))

    pone.close()
    one.close()
    two = ctx.enter_context(ExitStack())
    ptwo = ctx.enter_context(ExitStack())
    raw_w.append(sb("raw_w1", W_ALL, at=two))
    wh.append(sb("wh1", NWE, dt=F32R, at=two))
    wl.append(sb("wl1", NWE, dt=F32R, at=two))
    bias = [sb(f"bias{i}", 2, CH, at=two) for i in range(2)]
    b_down = [sb(f"b_down{i}", D, at=two) for i in range(2)]
    xq.append(sb("xq1", SUBS, ROW, at=two))
    tok = [sb(f"tok{i}", SUBS, dt=U32, at=two) for i in range(2)]
    share = [sb(f"share{i}", SUBS, at=two) for i in range(2)]
    xh = [sb(f"xh{i}", KD, TILE, dt=F32R, at=two) for i in range(2)]
    xl = [sb(f"xl{i}", KD, TILE, dt=F32R, at=two) for i in range(2)]
    gate_v = [sb(f"gate_v{i}", TILE, at=two) for i in range(2)]
    up_v = [sb(f"up_v{i}", TILE, at=two) for i in range(2)]
    sig = [sb(f"sig{i}", TILE, at=two) for i in range(2)]
    a_v = [sb(f"a_v{i}", TILE, at=two) for i in range(2)]
    ah = sb("ah", CH, TILE, dt=F32R, at=two)
    al = sb("al", CH, TILE, dt=F32R, at=two)
    o_v = [sb(f"o_v{i}", SUBS, D, at=two) for i in range(2)]

    p_x = [ps(f"p_x{i}", TILE, at=ptwo) for i in range(KD)]
    p_g = [ps(f"p_g{i}", TILE, at=ptwo) for i in range(2)]
    p_up = [ps(f"p_up{i}", TILE, at=ptwo) for i in range(2)]
    p_o = [ps(f"p_o{i}", 2 * D, at=ptwo) for i in range(2)]

    s_scrap2 = sem("s_scrap2")
    s_xh, s_xl = sem("s_xh"), sem("s_xl")
    s_g, s_up, s_prod, s_sig, s_a, s_ah, s_al = (sem(n) for n in ("s_g", "s_up", "s_prod", "s_sig", "s_a", "s_ah", "s_al"))
    s_o, s_scaled_o = sem("s_o"), sem("s_scaled_o")
    s_add = [sem(f"s_add{i}") for i in range(2)]
    ADDS = 16 * SUBS
    LAG = 2

    def last_pair(eng):
        return eng.value_load(pairs_i[0:1, 0:1], min_val=TOKENS * TOPK // TILE // 2 - 1, max_val=TILES // 2 - 1)

    def tiles(eng, last_p):
        for k in range(2):
            yield Seq(0, k)
        with eng.Fori(1, last_p + 1) as pair:
            for k in range(2):
                yield Seq(pair, k)

    def pe_stage2(pe):
        last_p = last_pair(pe)

        def transpose_tile(t):
            pe.wait_ge(s_rows[t.p], 16 * (t.use + 1))
            after(pe, s_xl, KD * t.n)
            for k in range(KD):
                for a in range(SUBS):
                    mm = pe.transpose(p_x[k][:, a * P:(a + 1) * P], xq[t.p][:, a, k * P:(k + 1) * P], ident[:, :])
                mm.then_inc(s_tr, 1)

        def up_projection(t, i):
            n = CH * t.n + i
            if i == 0:
                pe.wait_ge(s_xl, KD * (t.n + 1))
                pe.wait_ge(s_wl, 2 * t.n + 1)
            after(pe, s_up, n - 1)
            for to, at in ((p_g[i % 2], i * P), (p_up[i % 2], INNER + i * P)):
                for k in range(KD):
                    c = k * 2 * INNER + at
                    for m, (w, v) in enumerate(((wh, xh), (wh, xl), (wl, xh))):
                        mm = pe.matmul(to[:, :], w[t.p][:, c:c + P], v[t.p][:, k, :],
                                       start=(k == 0 and m == 0), stop=(k == KD - 1 and m == 2))
            mm.then_inc(s_gu, 1)

        def down_projection(t, i):
            n = CH * t.n + i
            if i == 0:
                pe.wait_ge(s_wl, 2 * t.n + 2)
                after(pe, s_o, 2 * t.n)
            pe.wait_ge(s_ah, n + 1)
            pe.wait_ge(s_al, n + 1)
            c = GU + i * D
            for a in range(SUBS):
                to = p_o[a // 2][:, (a % 2) * D:(a % 2 + 1) * D]
                for m, (v, w) in enumerate(((ah, wh), (ah, wl), (al, wh))):
                    mm = pe.matmul(to, v[:, i, a * P:(a + 1) * P], w[t.p][:, c:c + D],
                                   start=(i == 0 and a % 2 == 0 and m == 0), stop=(i == CH - 1 and m == 2),
                                   skip_group_check=True)
            mm.then_inc(s_down, 1)

        transpose_tile(Seq(0, 0))
        for t in tiles(pe, last_p):
            for i in range(CH):
                up_projection(t, i)
                if i == 0:
                    transpose_tile(t.at(1))
                if i < LAG and (t.off > 0 or not isinstance(t.half, int)):
                    down_projection(t.at(-1), i + CH - LAG)
            for i in range(CH - LAG):
                down_projection(t, i)
        end = Seq(last_p, 1)
        for i in range(LAG):
            down_projection(end, i + CH - LAG)

    def act_stage2(act):
        last_p = last_pair(act)

        def copy_tile(t, k):
            act.wait_ge(s_tr, KD * t.n + k + 1)
            if k == 0:
                after(act, s_gu, CH * (t.n - 1))
            act.activation(xh[t.p][:, k, :], p_x[k][:, :], ACT.Copy).then_inc(s_xh, 1)

        def sigmoid(t, i):
            n = CH * t.n + i
            act.wait_ge(s_g, n + 1)
            after(act, s_a, n - 1)
            act.activation(sig[i % 2][:, :], gate_v[i % 2][:, :], ACT.Sigmoid, scale=ALPHA).then_inc(s_sig, 1)

        def copy_product(t, i):
            n = CH * t.n + i
            act.wait_ge(s_a, n + 1)
            after(act, s_down, n - CH + 1)
            act.activation(ah[:, i, :], a_v[i % 2][:, :], ACT.Copy).then_inc(s_ah, 1)

        def copy_share(t, expert):
            act.wait_ge(s_rows[t.p], 16 * (t.use + 1))
            act.activation(share[t.p][:, :], xq[t.p][:, :, bass.ds(expert + COL_WEIGHT, 1)].rearrange("p a b -> p (a b)"),
                           ACT.Copy).then_inc(s_share, 1)

        def weigh_output(t):
            act.wait_ge(s_share, t.n + 1)
            for a in range(SUBS):
                if a % 2 == 0:
                    act.wait_ge(s_o, 2 * t.n + a // 2 + 1)
                last = act.activation(o_v[t.p][:, a, :], o_v[t.p][:, a, :], ACT.Copy, scale=share[t.p][:, a:a + 1])
            last.then_inc(s_scaled_o, 1)

        first_tile = Seq(0, 0)
        for k in range(KD):
            copy_tile(first_tile, k)
        for t in tiles(act, last_p):
            later = t.off > 0 or not isinstance(t.half, int)
            expert = act.value_load(expert_i[0:1, bass.ds(t.n, 1)], min_val=0, max_val=E - 1)
            for i in range(CH):
                if i > 0:
                    copy_product(t, i - 1)
                elif later:
                    copy_product(t.at(-1), CH - 1)
                sigmoid(t, i)
                if i == 0:
                    copy_share(t, expert)
                if i < 2:
                    copy_weights(act, t.at(1), i)
                if i == 1:
                    for k in range(KD):
                        copy_tile(t.at(1), k)
                if i == 2 and later:
                    weigh_output(t.at(-1))
                if i == 3:
                    copy_weights(act, t.at(1), 2)
        end = Seq(last_p, 1)
        copy_product(end, CH - 1)
        weigh_output(end)

    def dve_stage2(dve):
        last_p = last_pair(dve)

        def read_bias(t):
            dve.wait_ge(s_w[t.p], 16 * (t.use + 1))
            dve.tensor_copy(bias[t.p][:, 0, :], raw_w[t.p][:, NWE:NWE + CH])
            dve.tensor_scalar(bias[t.p][:, 1, :], raw_w[t.p][:, NWE + CH:NWE + 2 * CH], 1.0, None, ALU.add)
            dve.tensor_copy(b_down[t.p][:, :], raw_w[t.p][:, NWE + 2 * CH:W_ALL]).then_inc(s_bias, 1)

        def rest_of_tile(t, k):
            dve.wait_ge(s_xh, KD * t.n + k + 1)
            dve.tensor_tensor(xl[t.p][:, k, :], p_x[k][:, :], xh[t.p][:, k, :].bitcast(F32), ALU.subtract)\
               .then_inc(s_xl, 1)

        def read_chunk(t, i):
            n = CH * t.n + i
            dve.wait_ge(s_gu, n + 1)
            if i == 0:
                dve.wait_ge(s_bias, t.n + 1)
            dve.tensor_scalar(gate_v[i % 2][:, :], p_g[i % 2][:, :], bias[t.p][:, 0, i:i + 1], LIMIT, ALU.add, ALU.min)\
               .then_inc(s_g, 1)
            dve.tensor_scalar(up_v[i % 2][:, :], p_up[i % 2][:, :], bias[t.p][:, 1, i:i + 1], LIMIT + 1.0,
                              ALU.add, ALU.min).then_inc(s_up, 1)

        def rest_of_product(t, i):
            n = CH * t.n + i
            dve.wait_ge(s_ah, n + 1)
            dve.tensor_tensor(al[:, i, :], a_v[i % 2][:, :], ah[:, i, :].bitcast(F32), ALU.subtract).then_inc(s_al, 1)

        def product_of_chunk(t, i):
            n = CH * t.n + i
            dve.wait_ge(s_up, n + 1)
            dve.scalar_tensor_tensor(up_v[i % 2][:, :], up_v[i % 2][:, :], 1.0 - LIMIT, gate_v[i % 2][:, :],
                                     ALU.max, ALU.mult).then_inc(s_prod, 1)

        def times_sigmoid(t, i):
            n = CH * t.n + i
            dve.wait_ge(s_prod, n + 1)
            dve.wait_ge(s_sig, n + 1)
            dve.tensor_tensor(a_v[i % 2][:, :], up_v[i % 2][:, :], sig[i % 2][:, :], ALU.mult).then_inc(s_a, 1)

        def copy_tokens(t):
            dve.wait_ge(s_rows[t.p], 16 * (t.use + 1))
            after(dve, s_add[t.p], ADDS * t.use)
            dve.tensor_copy(tok[t.p][:, :], xq[t.p][:, :, COL_TOKEN].bitcast(I32)).then_inc(s_tok, 1)

        def read_output(t):
            for b in range(2):
                if b == 0:
                    dve.wait_ge(s_down, CH * (t.n + 1))
                dve.tensor_tensor(o_v[t.p][:, 2 * b:2 * b + 2, :], p_o[b][:, :].rearrange("p (a d) -> p a d", d=D),
                                  b_down[t.p][:, :].unsqueeze(1).broadcast_to([P, 2, D]), ALU.add).then_inc(s_o, 1)

        for k in range(KD):
            rest_of_tile(Seq(0, 0), k)
        read_bias(Seq(0, 0))
        for t in tiles(dve, last_p):
            later = t.off > 0 or not isinstance(t.half, int)
            for i in range(CH):
                read_chunk(t, i)
                product_of_chunk(t, i)
                if i > 0:
                    rest_of_product(t, i - 1)
                elif later:
                    rest_of_product(t.at(-1), CH - 1)
                if i == 2:
                    for k in range(KD):
                        rest_of_tile(t.at(1), k)
                times_sigmoid(t, i)
                if i == 1 and later:
                    read_output(t.at(-1))
                if i == 0:
                    copy_tokens(t)
                if i == 3:
                    read_bias(t.at(1))
        end = Seq(last_p, 1)
        rest_of_product(end, CH - 1)
        read_output(end)

    def pool_stage2(pool):
        last_p = last_pair(pool)

        def add_output(t):
            if t.off != 0 or not isinstance(t.half, int):
                last = t.at(-1)
                pool.wait_ge(s_add[last.p], ADDS * (last.use + 1))
            pool.wait_ge(s_tok, t.n + 1)
            pool.wait_ge(s_scaled_o, t.n + 1)
            after(pool, s_scrap2, t.n)
            pool.tensor_tensor(scrap[:, 1:2], neg_half[:, 0:1], neg_half[:, 0:1], ALU.mult).then_inc(s_scrap2, 1)
            for a in range(SUBS):
                pool.indirect_dma_start(total, bass.IndirectOffsetOnAxis(ap=tok[t.p][:, a:a + 1], axis=0),
                                        o_v[t.p][:, a, :], None, compute_op=ALU.add).then_inc(s_add[t.p], 16)

        rest_of_weights(pool, Seq(0, 0), 1)
        pool.wait_ge(s_pad, 16 * (E + 2))
        for t in tiles(pool, last_p):
            rest_of_weights(pool, t.at(1), 0)
            if t.off > 0 or not isinstance(t.half, int):
                add_output(t.at(-1))
            rest_of_weights(pool, t.at(1), 1)
        add_output(Seq(last_p, 1))

    def sp_stage2(sp):
        last_p = last_pair(sp)
        for t in tiles(sp, last_p):
            load_weights(sp, t.at(1))
            load_rows(sp, t.at(1))
        return last_p

    stage2_ends = []

    with nc.Block() as block:
        @block.tensor
        def _(pe):
            pe_stage2(pe)

        @block.scalar
        def _(act):
            act_stage2(act)

        @block.vector
        def _(dve):
            dve_stage2(dve)

        @block.gpsimd
        def _(pool):
            pool_stage2(pool)

        @block.sync
        def _(sp):
            last_p = sp_stage2(sp)
            waits = [(s_w[0], 16 * (last_p + 2)), (s_rows[0], 16 * (last_p + 2))]
            waits += [(s_add[i], ADDS * (last_p + 1)) for i in range(2)]
            stage2_ends.extend(waits)

    ptwo.close()
    two.close()
    three = ctx.enter_context(ExitStack())
    sums = [sb(f"sums{i}", TT, D, at=three) for i in range(SEQS)]
    stats3 = sb("stats3", SEQS, TT, 6, at=three)
    mv3 = sb("mv3", SEQS, TT, 2, at=three)
    rstd3 = sb("rstd3", SEQS, TT, at=three)
    neg_mean3 = sb("neg_mean3", SEQS, TT, at=three)
    s_sums = [sem(f"s_sums{i}") for i in range(SEQS)]
    s_stats3, s_mv3, s_eps3, s_pow3, s_rstd3, s_normed, s_store = (
        sem(n) for n in ("s_stats3", "s_mv3", "s_eps3", "s_pow3", "s_rstd3", "s_normed", "s_store"))

    with nc.Block() as block:
        @block.sync
        def _(sp):
            for s_done, n in stage2_ends:
                sp.wait_ge(s_done, n)
            for s in range(SEQS):
                sp.dma_start(sums[s][:, :, :], total_rows[s]).then_inc(s_sums[s], 16)

        @block.vector
        def _(dve):
            for s in range(SEQS + 2):
                if s < SEQS:
                    dve.wait_ge(s_sums[s], 16)
                    for t in range(TT):
                        last = dve.bn_stats(stats3[:, s, t, :], sums[s][:, t, :])
                    last.then_inc(s_stats3, 1)
                if 0 <= s - 1 < SEQS:
                    dve.wait_ge(s_stats3, s)
                    for t in range(TT):
                        last = dve.bn_aggr(mv3[:, s - 1, t, :], stats3[:, s - 1, t, :])
                    last.then_inc(s_mv3, 1)
                if s >= 2:
                    dve.wait_ge(s_mv3, s - 1)
                    dve.tensor_scalar(mv3[:, s - 2, :, 1], mv3[:, s - 2, :, 1], EPS, None, ALU.add)
                    dve.tensor_scalar(neg_mean3[:, s - 2, :], mv3[:, s - 2, :, 0], -1.0, None, ALU.mult)\
                       .then_inc(s_eps3, 1)

        @block.gpsimd
        def _(pool):
            for s in range(SEQS):
                pool.wait_ge(s_eps3, s + 1)
                pool.tensor_tensor(rstd3[:, s, :], mv3[:, s, :, 1], neg_half[:, :], ALU.pow).then_inc(s_pow3, 1)
                pool.wait_ge(s_pow3, s + 1)
                pool.tensor_tensor(neg_mean3[:, s, :], neg_mean3[:, s, :], rstd3[:, s, :], ALU.mult).then_inc(s_rstd3, 1)

        @block.scalar
        def _(act):
            for s in range(SEQS):
                act.wait_ge(s_rstd3, s + 1)
                for t in range(TT):
                    last = act.activation(sums[s][:, t, :], sums[s][:, t, :], ACT.Identity,
                                          bias=neg_mean3[:, s, t:t + 1], scale=rstd3[:, s, t:t + 1])
                last.then_inc(s_normed, 1)
                act.wait_ge(s_normed, s + 1)
                act.dma_start(out_rows[s], sums[s][:, :, :]).then_inc(s_store, 16)
            act.wait_ge(s_store, 16 * SEQS)


def kernel(**inputs):
    import concourse.bacc as bacc
    from concourse.bass_utils import run_bass_kernel_spmd

    i = {k.split("_", 2)[2] if k.startswith("L0_attn") else k[3:]: np.asarray(v) for k, v in inputs.items()}
    x = np.ascontiguousarray(i["x"])

    def cols(v):
        return np.ascontiguousarray(v.reshape(-1, P).T)

    def rows(v):
        return np.ascontiguousarray(np.broadcast_to(v, (P, v.size)))

    small = {
        **CONSTANTS,
        "wr": np.ascontiguousarray(i["ffn_router_weight"].T.reshape(KD, P, E).transpose(1, 0, 2)),
        "rate": np.ascontiguousarray(i["A_log"].reshape(GROUPS, P).T),
        "b_in": cols(i["in_proj_b"]),
        "b_conv": cols(i["conv_b"]),
        "b_dt": cols(i["dt_b"]),
        "skip": cols(i["D"]),
        "b_bc": np.ascontiguousarray(np.tile(i["bc_b"].reshape(2, STATE), (1, CHPG)).T),
        "taps": np.ascontiguousarray(i["conv_w"].reshape(HALVES, P, TAPS).transpose(1, 0, 2)),
        "ln_g": rows(i["ln_g"]),
        "ln_b": rows(i["ln_b"]),
        "b_router": rows(i["ffn_router_bias"]),
    }
    arrays = {
        "x": x,
        "x_t": np.ascontiguousarray(x.transpose(0, 2, 1)),
        "weights": np.concatenate([i["in_proj_w"].T, i["dt_w"].T, i["out_w"].T, i["bc_w"].T], axis=1).reshape(KD, P, NW),
        "small": np.concatenate([small[name].reshape(P, -1) for name, *_ in SMALL], axis=1),
        "set_up": np.concatenate([CONSTANTS["before"], CONSTANTS["ones"], np.broadcast_to(i["out_b"], (P, D))], axis=1),
        "pick": CONSTANTS["pick"],
        "tile": CONSTANTS["tile"],
        "w_experts": np.concatenate([
            i["ffn_gate_up_proj"].reshape(E, 2 * INNER, KD, P).transpose(0, 3, 2, 1).reshape(E, P, -1),
            i["ffn_down_proj"].reshape(E, D, CH, P).transpose(0, 3, 2, 1).reshape(E, P, -1),
            i["ffn_gate_up_proj_bias"].reshape(E, 2 * CH, P).transpose(0, 2, 1),
            np.broadcast_to(i["ffn_down_proj_bias"][:, None, :], (E, P, D))], axis=2),
    }
    nc = bacc.Bacc("TRN2", target_bir_lowering=False, num_devices=1)
    ins = {k: nc.dram_tensor(f"in_{k}", a.shape, mybir.dt.from_np(a.dtype), kind="ExternalInput").ap()
           for k, a in arrays.items()}
    out = nc.dram_tensor("out", (SEQS, LEN, D), F32, kind="ExternalOutput").ap()
    program(nc, ins, out)
    r = run_bass_kernel_spmd(nc, [{f"in_{k}": a for k, a in arrays.items()}], core_ids=[0])
    return r.results[0]["out"]
```
